# Optimizing a Trainium2 kernel written in Bass

```python
import numpy as np
import jax
import jax.numpy as jnp

def _softmax(x, axis=-1):
    return jax.nn.softmax(x, axis=axis)

def _gelu(x):
    return jax.nn.gelu(x, approximate=True)

def _silu(x):
    return jax.nn.silu(x)

def _sigmoid(x):
    return jax.nn.sigmoid(x)

def _layernorm(x, axis=-1, eps=1e-05):
    m = jnp.mean(x, axis=axis, keepdims=True)
    v = jnp.var(x, axis=axis, keepdims=True)
    return (x - m) / jnp.sqrt(v + eps)

def _scatter_add(tgt, idx, src, axis=0):
    return tgt.at[idx].add(src)

def _segment_sum(src, seg, n):
    return jax.ops.segment_sum(src, seg, n)
kernel_name = 'mk_dlrm_tower_d1_rec_r8_1721f5'

def setup_inputs(seed: int=0):
    np.random.seed(seed)
    _w = jnp.asarray

    def _rec_inputs():
        import jax
        import jax.numpy as jnp
        _tk = jax.random.key(seed)
        ids = jnp.stack([jax.random.randint(jax.random.fold_in(_tk, 200 + f), (2048,), 0, v, jnp.int32) for f, v in enumerate([12500, 125000, 12500, 1250, 12500, 125000, 125000, 1000, 12500, 12500, 1250, 1250, 1250, 1250, 12500, 12500, 12500, 1250, 1250, 1000, 1000, 1000, 1000, 1000, 1000, 1000])], axis=1)
        tbl_0 = 0.05 * jax.random.normal(jax.random.fold_in(_tk, 500 + 0), (12500, 64), jnp.float32)
        tbl_1 = 0.05 * jax.random.normal(jax.random.fold_in(_tk, 500 + 1), (125000, 64), jnp.float32)
        tbl_2 = 0.05 * jax.random.normal(jax.random.fold_in(_tk, 500 + 2), (12500, 64), jnp.float32)
        tbl_3 = 0.05 * jax.random.normal(jax.random.fold_in(_tk, 500 + 3), (1250, 64), jnp.float32)
        tbl_4 = 0.05 * jax.random.normal(jax.random.fold_in(_tk, 500 + 4), (12500, 64), jnp.float32)
        tbl_5 = 0.05 * jax.random.normal(jax.random.fold_in(_tk, 500 + 5), (125000, 64), jnp.float32)
        tbl_6 = 0.05 * jax.random.normal(jax.random.fold_in(_tk, 500 + 6), (125000, 64), jnp.float32)
        tbl_7 = 0.05 * jax.random.normal(jax.random.fold_in(_tk, 500 + 7), (1000, 64), jnp.float32)
        tbl_8 = 0.05 * jax.random.normal(jax.random.fold_in(_tk, 500 + 8), (12500, 64), jnp.float32)
        tbl_9 = 0.05 * jax.random.normal(jax.random.fold_in(_tk, 500 + 9), (12500, 64), jnp.float32)
        tbl_10 = 0.05 * jax.random.normal(jax.random.fold_in(_tk, 500 + 10), (1250, 64), jnp.float32)
        tbl_11 = 0.05 * jax.random.normal(jax.random.fold_in(_tk, 500 + 11), (1250, 64), jnp.float32)
        tbl_12 = 0.05 * jax.random.normal(jax.random.fold_in(_tk, 500 + 12), (1250, 64), jnp.float32)
        tbl_13 = 0.05 * jax.random.normal(jax.random.fold_in(_tk, 500 + 13), (1250, 64), jnp.float32)
        tbl_14 = 0.05 * jax.random.normal(jax.random.fold_in(_tk, 500 + 14), (12500, 64), jnp.float32)
        tbl_15 = 0.05 * jax.random.normal(jax.random.fold_in(_tk, 500 + 15), (12500, 64), jnp.float32)
        tbl_16 = 0.05 * jax.random.normal(jax.random.fold_in(_tk, 500 + 16), (12500, 64), jnp.float32)
        tbl_17 = 0.05 * jax.random.normal(jax.random.fold_in(_tk, 500 + 17), (1250, 64), jnp.float32)
        tbl_18 = 0.05 * jax.random.normal(jax.random.fold_in(_tk, 500 + 18), (1250, 64), jnp.float32)
        tbl_19 = 0.05 * jax.random.normal(jax.random.fold_in(_tk, 500 + 19), (1000, 64), jnp.float32)
        tbl_20 = 0.05 * jax.random.normal(jax.random.fold_in(_tk, 500 + 20), (1000, 64), jnp.float32)
        tbl_21 = 0.05 * jax.random.normal(jax.random.fold_in(_tk, 500 + 21), (1000, 64), jnp.float32)
        tbl_22 = 0.05 * jax.random.normal(jax.random.fold_in(_tk, 500 + 22), (1000, 64), jnp.float32)
        tbl_23 = 0.05 * jax.random.normal(jax.random.fold_in(_tk, 500 + 23), (1000, 64), jnp.float32)
        tbl_24 = 0.05 * jax.random.normal(jax.random.fold_in(_tk, 500 + 24), (1000, 64), jnp.float32)
        tbl_25 = 0.05 * jax.random.normal(jax.random.fold_in(_tk, 500 + 25), (1000, 64), jnp.float32)
        _rk = jax.random.fold_in(_tk, 7)
        r_dense_t = 7.22013e-05 + 1.00017 * jax.random.normal(jax.random.fold_in(_rk, 101), (2048, 256), jnp.float32)
        W_top1 = 0.0360844 * jax.random.normal(jax.random.fold_in(_tk, 801), (768, 512), jnp.float32)
        W_top2 = 0.0441942 * jax.random.normal(jax.random.fold_in(_tk, 802), (512, 256), jnp.float32)
        W_top3 = 0.0625 * jax.random.normal(jax.random.fold_in(_tk, 803), (256, 1), jnp.float32)
        b_top1 = jnp.zeros((512,), jnp.float32)
        b_top2 = jnp.zeros((256,), jnp.float32)
        return (r_dense_t, ids, tbl_0, tbl_1, tbl_2, tbl_3, tbl_4, tbl_5, tbl_6, tbl_7, tbl_8, tbl_9, tbl_10, tbl_11, tbl_12, tbl_13, tbl_14, tbl_15, tbl_16, tbl_17, tbl_18, tbl_19, tbl_20, tbl_21, tbl_22, tbl_23, tbl_24, tbl_25, W_top1, b_top1, W_top2, b_top2, W_top3)
    r_dense_t, ids, tbl_0, tbl_1, tbl_2, tbl_3, tbl_4, tbl_5, tbl_6, tbl_7, tbl_8, tbl_9, tbl_10, tbl_11, tbl_12, tbl_13, tbl_14, tbl_15, tbl_16, tbl_17, tbl_18, tbl_19, tbl_20, tbl_21, tbl_22, tbl_23, tbl_24, tbl_25, W_top1, b_top1, W_top2, b_top2, W_top3 = _rec_inputs()

    def _L0_rec_setup():
        import jax, jax.numpy as jnp
        import numpy as np
        EPS = 1e-05
        NI = 33
        TRIL_I, TRIL_J = np.tril_indices(NI, k=-1)

        def layer_norm(x, g, b):
            m = jnp.mean(x, axis=-1, keepdims=True)
            v = jnp.mean(jnp.square(x - m), axis=-1, keepdims=True)
            return (x - m) * jax.lax.rsqrt(v + EPS) * g + b
        key = jax.random.key(seed)
        ks = jax.random.split(key, 8)
        B, D_DENSE, N_SP, D_SP = (4096, 256, 26, 64)
        E, PROJ, MAXD, NFLAT = (128, 32, 512, 528)
        dense_t = jax.random.normal(ks[0], (B, D_DENSE), dtype=jnp.float32)
        sparse_t = jax.random.normal(ks[1], (B, N_SP, D_SP), dtype=jnp.float32)
        Wd = jax.random.normal(ks[2], (E, D_DENSE), dtype=jnp.float32) / np.sqrt(D_DENSE)
        Ws = jax.random.normal(ks[3], (E, D_SP), dtype=jnp.float32) / np.sqrt(D_SP)
        Wsi = jax.random.normal(ks[4], (PROJ, N_SP), dtype=jnp.float32) / np.sqrt(N_SP)
        Wl = jax.random.normal(ks[5], (MAXD, NFLAT), dtype=jnp.float32) / np.sqrt(NFLAT)
        gd = jnp.ones((E,), jnp.float32)
        bd = jnp.zeros((E,), jnp.float32)
        gs = jnp.ones((E,), jnp.float32)
        bs = jnp.zeros((E,), jnp.float32)
        gsi = jnp.ones((PROJ,), jnp.float32)
        bsi = jnp.zeros((PROJ,), jnp.float32)
        gl = jnp.ones((MAXD,), jnp.float32)
        bl = jnp.zeros((MAXD,), jnp.float32)
        return {'dense_t': dense_t, 'sparse_t': sparse_t, 'Wd': Wd, 'gd': gd, 'bd': bd, 'Ws': Ws, 'gs': gs, 'bs': bs, 'Wsi': Wsi, 'gsi': gsi, 'bsi': bsi, 'Wl': Wl, 'gl': gl, 'bl': bl, 'dims_in_use': 384}
    _L0_rec_all = _L0_rec_setup()
    _L0_rec_in = {k: v for k, v in _L0_rec_all.items() if k in ('Wd', 'gd', 'bd', 'Ws', 'gs', 'bs', 'Wsi', 'gsi', 'bsi', 'Wl', 'gl', 'bl')}
    del _L0_rec_all
    return {'r_dense_t': r_dense_t, 'ids': ids, 'tbl_0': tbl_0, 'tbl_1': tbl_1, 'tbl_2': tbl_2, 'tbl_3': tbl_3, 'tbl_4': tbl_4, 'tbl_5': tbl_5, 'tbl_6': tbl_6, 'tbl_7': tbl_7, 'tbl_8': tbl_8, 'tbl_9': tbl_9, 'tbl_10': tbl_10, 'tbl_11': tbl_11, 'tbl_12': tbl_12, 'tbl_13': tbl_13, 'tbl_14': tbl_14, 'tbl_15': tbl_15, 'tbl_16': tbl_16, 'tbl_17': tbl_17, 'tbl_18': tbl_18, 'tbl_19': tbl_19, 'tbl_20': tbl_20, 'tbl_21': tbl_21, 'tbl_22': tbl_22, 'tbl_23': tbl_23, 'tbl_24': tbl_24, 'tbl_25': tbl_25, 'W_top1': W_top1, 'b_top1': b_top1, 'W_top2': W_top2, 'b_top2': b_top2, 'W_top3': W_top3, 'L0_rec_Wd': _L0_rec_in['Wd'], 'L0_rec_gd': _L0_rec_in['gd'], 'L0_rec_bd': _L0_rec_in['bd'], 'L0_rec_Ws': _L0_rec_in['Ws'], 'L0_rec_gs': _L0_rec_in['gs'], 'L0_rec_bs': _L0_rec_in['bs'], 'L0_rec_Wsi': _L0_rec_in['Wsi'], 'L0_rec_gsi': _L0_rec_in['gsi'], 'L0_rec_bsi': _L0_rec_in['bsi'], 'L0_rec_Wl': _L0_rec_in['Wl'], 'L0_rec_gl': _L0_rec_in['gl'], 'L0_rec_bl': _L0_rec_in['bl']}

def reference(r_dense_t, ids, tbl_0, tbl_1, tbl_2, tbl_3, tbl_4, tbl_5, tbl_6, tbl_7, tbl_8, tbl_9, tbl_10, tbl_11, tbl_12, tbl_13, tbl_14, tbl_15, tbl_16, tbl_17, tbl_18, tbl_19, tbl_20, tbl_21, tbl_22, tbl_23, tbl_24, tbl_25, W_top1, b_top1, W_top2, b_top2, W_top3, L0_rec_Wd, L0_rec_gd, L0_rec_bd, L0_rec_Ws, L0_rec_gs, L0_rec_bs, L0_rec_Wsi, L0_rec_gsi, L0_rec_bsi, L0_rec_Wl, L0_rec_gl, L0_rec_bl):
    import jax
    import jax.numpy as jnp

    def _L0_rec_ref(dense_t, sparse_t, Wd, gd, bd, Ws, gs, bs, Wsi, gsi, bsi, Wl, gl, bl, dims_in_use):
        import jax, jax.numpy as jnp
        import numpy as np
        EPS = 1e-05
        NI = 33
        TRIL_I, TRIL_J = np.tril_indices(NI, k=-1)

        def layer_norm(x, g, b):
            m = jnp.mean(x, axis=-1, keepdims=True)
            v = jnp.mean(jnp.square(x - m), axis=-1, keepdims=True)
            return (x - m) * jax.lax.rsqrt(v + EPS) * g + b
        x = layer_norm(dense_t @ Wd.T, gd, bd)
        y = layer_norm(jnp.einsum('bnd,ed->bne', sparse_t, Ws), gs, bs)
        y = jnp.einsum('bne,pn->bep', y, Wsi)
        y = layer_norm(y, gsi, bsi)
        y = jnp.swapaxes(y, 1, 2)
        T = jnp.concatenate([x[:, None, :], y], axis=1)
        Z = jnp.einsum('bnd,bmd->bnm', T, T)
        Zflat = Z[:, TRIL_I, TRIL_J]
        out = layer_norm(Zflat @ Wl.T, gl, bl)
        maxd = out.shape[-1]
        mask = (jnp.arange(maxd) < dims_in_use).astype(out.dtype)
        return out * mask
    e = jnp.stack([tbl_0[ids[:, 0]], tbl_1[ids[:, 1]], tbl_2[ids[:, 2]], tbl_3[ids[:, 3]], tbl_4[ids[:, 4]], tbl_5[ids[:, 5]], tbl_6[ids[:, 6]], tbl_7[ids[:, 7]], tbl_8[ids[:, 8]], tbl_9[ids[:, 9]], tbl_10[ids[:, 10]], tbl_11[ids[:, 11]], tbl_12[ids[:, 12]], tbl_13[ids[:, 13]], tbl_14[ids[:, 14]], tbl_15[ids[:, 15]], tbl_16[ids[:, 16]], tbl_17[ids[:, 17]], tbl_18[ids[:, 18]], tbl_19[ids[:, 19]], tbl_20[ids[:, 20]], tbl_21[ids[:, 21]], tbl_22[ids[:, 22]], tbl_23[ids[:, 23]], tbl_24[ids[:, 24]], tbl_25[ids[:, 25]]], axis=1)
    z = _L0_rec_ref(r_dense_t, e, L0_rec_Wd, L0_rec_gd, L0_rec_bd, L0_rec_Ws, L0_rec_gs, L0_rec_bs, L0_rec_Wsi, L0_rec_gsi, L0_rec_bsi, L0_rec_Wl, L0_rec_gl, L0_rec_bl, 384)
    z = z.reshape(z.shape[0], -1)
    h = jnp.concatenate([z, r_dense_t], axis=1)
    h = jnp.maximum(h @ W_top1 + b_top1, 0.0)
    h = jnp.maximum(h @ W_top2 + b_top2, 0.0)
    y = h @ W_top3
    return y

_drawn_inputs = setup_inputs


def setup_inputs(seed=0):
    import zlib

    import numpy as np

    out = dict(_drawn_inputs(seed))
    spreads = {'b_top1': (0.0, 0.1),
     'b_top2': (0.0, 0.1),
     'L0_rec_gd': (1.0, 0.6),
     'L0_rec_bd': (0.0, 0.8),
     'L0_rec_gs': (1.0, 0.6),
     'L0_rec_bs': (0.0, 0.1),
     'L0_rec_gsi': (1.0, 0.2),
     'L0_rec_bsi': (0.0, 0.1),
     'L0_rec_gl': (1.0, 0.2),
     'L0_rec_bl': (0.0, 0.1)}
    factors = {}
    for name, (base, spread) in spreads.items():
        noise = np.random.default_rng([zlib.crc32(name.encode()), seed]).standard_normal(out[name].shape)
        drawn = base * np.exp(spread * noise) if base else spread * noise
        out[name] = jnp.asarray(drawn.astype(out[name].dtype))
    for name, factor in factors.items():
        out[name] = (out[name] * factor).astype(out[name].dtype)
    return out
```

```python
from contextlib import ExitStack

import numpy as np

import concourse.bass as bass
from concourse import mybir

ALU = mybir.AluOpType
ACT = mybir.ActivationFunctionType
AX = mybir.AxisListType
F32 = mybir.dt.float32
I32 = mybir.dt.int32
F16 = mybir.dt.float16

P = 128
VOCAB = [12500, 125000, 12500, 1250, 12500, 125000, 125000, 1000, 12500, 12500, 1250, 1250, 1250,
         1250, 12500, 12500, 12500, 1250, 1250, 1000, 1000, 1000, 1000, 1000, 1000, 1000]
B = 2048
NS = len(VOCAB)
D = 64
DD = 256
E = 128
PR = 32
O = 512
OU = 384
H1, H2 = 512, 256
EPS = 1e-5

TILES = B // P
HALF = P // 2
CH = HALF * NS // P
SPAN = 6
BS = 16
BLOCKS = P // BS
GR = P // 4
SL = PR // 2
QK = SL // 4
TC = PR + 2
KD, KO, KH1, KH2 = DD // P, OU // P, H1 // P, H2 // P

GROUPS = [range(0, 4), range(4, 8), range(8, 12), range(12, 13)]
NG = len(GROUPS)


def samples_of(k):
    return k * P // NS, (k * P + P - 1) // NS


def fold_plan(m):
    plan = []
    for k in range(CH):
        a, b = samples_of(k)
        a, b = max(a, m * BS), min(b, m * BS + BS - 1)
        if a <= b:
            plan.append((k, a, b - a + 1))
    return plan


FOLDS = [fold_plan(m) for m in range(HALF // BS)]
NF = len(FOLDS)


def count(step, lag, per_tile, k):
    if isinstance(step, int):
        return (step - lag) * per_tile + k
    pair, odd = step
    return pair * (2 * per_tile) + ((odd - lag) * per_tile + k)


def await_(eng, sem, value):
    if isinstance(value, int) and value <= 0:
        return
    eng.wait_ge(sem, value)


def parity(step):
    return step % 2 if isinstance(step, int) else step[1]


def run_steps(eng, step_fn):
    for i in range(4):
        step_fn(i, True, i >= 1, i >= 2)
    with eng.Fori(2, TILES // 2) as pair:
        step_fn((pair, 0), True, True, True)
        step_fn((pair, 1), True, True, True)
    step_fn(TILES, False, True, True)
    step_fn(TILES + 1, False, False, True)


def build_tower(nc, table, ids, offsets, dense_t, ident, ws_t, gs, bs, wsi, owner, wd_t, gd, bd,
                wl, gsi_p, gsi_q, bsi_p, bsi_q, eye_p, eye_q, w1, gl, bl, b1, w2, b2, w3, upper, out):
    with ExitStack() as ctx:
        def sb(name, shape, dt=F32):
            return ctx.enter_context(nc.sbuf_tensor(name, shape, dt))

        def sem(name):
            return ctx.enter_context(nc.semaphore(name))

        bank = [ctx.enter_context(nc.psum_tensor(f"bank{n}", [P, 512], F32)) for n in range(8)]
        feat_bank = bank[0:2]
        fold_bank = bank[2:4]
        y_bank = bank[4:6]
        gram_bank = bank[6:8]

        identity = sb("identity", [P, P])
        eps = sb("eps", [P, 1])
        ones = sb("ones", [P, PR])
        ids_all = sb("ids_all", [P, TILES * 2 * CH], I32)
        off_sb = sb("off_sb", [P, 2 * CH], I32)
        ws_sb = sb("ws_sb", [P, E])
        gs_sb = sb("gs_sb", [P, E])
        wg_sb = sb("wg_sb", [P, E])
        ws_e = sb("ws_e", [P, P])
        gram_w = sb("gram_w", [P, P])
        wg_hi, wg_lo = sb("wg_hi", [P, E], F16), sb("wg_lo", [D, E], F16)
        bs_row = sb("bs_row", [1, E])
        wsum_row = sb("wsum_row", [1, BS, PR])
        bs_parts = sb("bs_parts", [1, 2, E], F16)
        wsum_parts = sb("wsum_parts", [1, 2, BS * PR], F16)
        bias_w = sb("bias_w", [3, E], F16)
        bias_m = sb("bias_m", [3, BS * PR], F16)
        wsi_sb = sb("wsi_sb", [P, CH, PR])
        owner_sb = sb("owner_sb", [P, CH, SPAN])
        fold_w = sb("fold_w", [P, CH, SPAN, PR])
        wd_sb = sb("wd_sb", [P, KD, E])
        gd_sb, bd_sb = sb("gd_sb", [P, 1]), sb("bd_sb", [P, 1])
        wl_sb = sb("wl_sb", [P, QK + 1, O])
        gp, gq = sb("gp", [P, 1]), sb("gq", [P, QK])
        bp, bq = sb("bp", [P, 1]), sb("bq", [P, QK])
        gg, gb, bg, bb = (sb(n, [P, QK]) for n in ("gg", "gb", "bg", "bb"))
        eye_p_sb = sb("eye_p_sb", [P, PR])
        eye_q_sb = sb("eye_q_sb", [P, QK, PR])
        take_upper = sb("take_upper", [P, SL], I32)
        mix_w = sb("mix_w", [P, QK + 1, P])
        w1_sb = sb("w1_sb", [P, KO + KD, H1])
        gl_sb, bl_sb = sb("gl_sb", [P, KO]), sb("bl_sb", [P, KO])
        b1_sb, b2_sb = sb("b1_sb", [P, KH1]), sb("b2_sb", [P, KH2])
        w2_sb = sb("w2_sb", [P, KH1, H2])
        w3_sb = sb("w3_sb", [P, KH2])
        mean_a, mean_b = sb("mean_a", [P, 1]), sb("mean_b", [P, CH])
        mean_c, mean_d = sb("mean_c", [P, KD]), sb("mean_d", [P, QK + 1])
        dense_all = sb("dense_all", [P, KD, B])

        wait_carrier_v = sb("wait_carrier_v", [P, 4])
        wait_carrier = sb("wait_carrier", [P, 1], I32)
        rows_id = [sb(f"rows_id{n}", [P, 2 * CH], I32) for n in range(2)]
        emb = [sb(f"emb{n}", [P, CH, 2, D]) for n in range(2)]
        dense_in = [sb(f"dense_in{n}", [P, KD, P]) for n in range(2)]
        emb_t = sb("emb_t", [P, CH, P])
        prod = sb("prod", [P, CH, 2, D])
        var1, std1, rstd1 = (sb(n, [P, CH, 2]) for n in ("var1", "std1", "rstd1"))
        emb_n = sb("emb_n", [P, CH, 2, D])
        junk_x = sb("junk_x", [P, E])
        var_x, std_x, rstd_x = (sb(n, [P, 1]) for n in ("var_x", "std_x", "rstd_x"))
        x_n = sb("x_n", [P, E])
        folded = sb("folded", [P, 2, NF, BS * PR], F16)
        square = [sb(f"square{n}", [P, BS, PR]) for n in range(2)]
        var2 = [sb(f"var2_{n}", [P, BS]) for n in range(2)]
        std2 = [sb(f"std2_{n}", [P, BS]) for n in range(2)]
        rstd2 = [sb(f"rstd2_{n}", [P, BS]) for n in range(2)]
        tt = [sb(f"tt{n}", [P, P, TC]) for n in range(2)]
        gram_s = sb("gram_s", [P, 4, GR, QK + 1])
        pairs = sb("pairs", [P, 4, GR, QK + 1])
        junk_z = sb("junk_z", [P, O])
        var3, std3, rstd3 = (sb(n, [P, 1]) for n in ("var3", "std3", "rstd3"))
        z_n = sb("z_n", [P, OU])
        z_t = sb("z_t", [P, KO, P])
        h1_t = sb("h1_t", [P, KH1, P])
        h2_t = sb("h2_t", [P, KH2, P])
        y_all = sb("y_all", [1, B])

        s_ids, s_small, s_ws, s_wsi, s_wl, s_w1, s_dense = (
            sem(n) for n in ("ids_in", "small_in", "ws_in", "wsi_in", "wl_in", "w1_in", "dense_in_all"))
        dense_got = [sem(f"dense_got{n}") for n in range(2)]
        s_ids_ready, s_prep, s_ws_ready, s_wse_ps, s_wse, s_gram_ps, s_gramw = (
            sem(n) for n in ("ids_ready", "prep_step", "ws_ready", "wse_ps", "wse", "gramw_ps", "gramw"))
        s_wsi_ready, s_wsum_ps, s_fold_ready, s_wd_ready = (
            sem(n) for n in ("wsi_ready", "wsum_ps", "fold_ready", "wd_ready"))
        s_mix_ready, s_mix_ps, s_wl_ready, s_b1_ps, s_w1_ready, s_const, s_parts, s_bias = (
            sem(n) for n in ("mix_ready", "mix_ps", "wl_ready", "b1_ps", "w1_ready", "const_ready",
                             "parts_ready", "bias_rows_in"))
        slot_ids = sem("slot_ids")
        gathered = [sem(f"gathered{n}") for n in range(2)]
        turned, turned_out = sem("turned"), sem("turned_out")
        x_sq, x_std, x_rstd, x_scaled, x_done = (
            sem(n) for n in ("x_sq", "x_std", "x_rstd", "x_scaled", "x_done"))
        g_done, prod_done = sem("g_done"), sem("prod_done")
        var1_done, std1_done, rstd1_done, emb_scaled = (
            sem(n) for n in ("var1_done", "std1_done", "rstd1_done", "emb_scaled"))
        fold_done, fold_out = sem("fold_done"), sem("fold_out")
        fold_high = sem("fold_high")
        y_done, sq_done, var_done, std_done, rstd_done, norm_done, gram_done = (
            sem(n) for n in ("y_done", "sq_done", "var_done", "std_done", "rstd_done", "norm_done",
                             "gram_done"))
        gram_low, gram_out = sem("gram_low"), sem("gram_out")
        regrouped = sem("regrouped")
        z_done, z_sq, z_std, z_rstd, z_scaled, zt_done, zt_out = (
            sem(n) for n in ("z_done", "z_sq", "z_std", "z_rstd", "z_scaled", "zt_done", "zt_out"))
        h1_done, h1_out, h2_done, h2_out, yv_done, yv_out = (
            sem(n) for n in ("h1_done", "h1_out", "h2_done", "h2_out", "yv_done", "yv_out"))
        stored = sem("stored")

        SMALL = [(identity, ident), (gd_sb, gd), (bd_sb, bd), (gp, gsi_p), (gq, gsi_q), (bp, bsi_p),
                 (bq, bsi_q), (eye_p_sb, eye_p), (eye_q_sb, eye_q), (gl_sb, gl), (bl_sb, bl),
                 (b1_sb, b1), (b2_sb, b2), (w3_sb, w3), (take_upper, upper)]
        WS = [(ws_sb, ws_t), (gs_sb, gs), (bs_row, bs)]
        WSI = [(wsi_sb, wsi), (owner_sb, owner), (wd_sb, wd_t)]
        dense_tiles = dense_t.rearrange("(c k) b -> k c b", k=P)

        block = ctx.enter_context(nc.Block())

        @block.sync
        def _(sp):
            sp.dma_start(ids_all[:], ids[:, :]).then_inc(s_ids, 16)
            sp.dma_start(off_sb[:], offsets[:, :]).then_inc(s_ids, 16)
            for dst, src in WS:
                sp.dma_start(dst[:], src).then_inc(s_ws, 16)
            for dst, src in SMALL:
                sp.dma_start(dst[:], src).then_inc(s_small, 16)
            for dst, src in WSI:
                sp.dma_start(dst[:], src).then_inc(s_wsi, 16)
            sp.dma_start(dense_in[0][:], dense_tiles[:, :, 0:P]).then_inc(dense_got[0], 16)
            sp.dma_start(wl_sb[:], wl).then_inc(s_wl, 16)
            sp.dma_start(w1_sb[:], w1).then_inc(s_w1, 16)
            sp.dma_start(w2_sb[:], w2).then_inc(s_w1, 16)
            sp.dma_start(dense_all[:], dense_tiles).then_inc(s_dense, 16)

            sp.wait_ge(s_parts, 1)
            for row, (u, v) in enumerate([(0, 0), (0, 1), (1, 0)]):
                sp.dma_start(bias_w[row:row + 1, :], bs_parts[:, u, :]).then_inc(s_bias, 16)
                sp.dma_start(bias_m[row:row + 1, :], wsum_parts[:, v, :]).then_inc(s_bias, 16)

            def held(value):
                return value if isinstance(value, int) else sp.snap(value)

            def step(i, a, c, t):
                nxt = i + 1 if isinstance(i, int) else i[0] * 2 + (i[1] + 1)
                if not isinstance(i, int) or nxt < TILES:
                    first, free = held(nxt * P), held(count(i, 0, NG, 0))
                    await_(sp, turned, free)
                    dst = dense_in[1 - parity(i)]
                    sp.dma_start(dst[:], dense_tiles[:, :, bass.ds(first, P)]).then_inc(
                        dense_got[1 - parity(i)], 16)
                if c:
                    await_(sp, gram_out, count(i, 1, 4, 4))
                    for j in range(4):
                        for r in range(4):
                            sp.dma_start(pairs[32 * r:32 * r + 32, j, :, :],
                                         gram_s[32 * j:32 * j + 32, r, :, :]).then_inc(regrouped, 16)

            for i in range(4):
                step(i, True, i >= 1, i >= 2)
            with sp.Fori(2, TILES // 2 - 1) as pair:
                step((pair, 0), True, True, True)
                step((pair, 1), True, True, True)
            step(TILES - 2, True, True, True)
            step(TILES - 1, True, True, True)
            step(TILES, False, True, True)
            sp.wait_ge(yv_out, TILES)
            sp.dma_start(out.rearrange("n o -> o n"), y_all[:]).then_inc(stored, 16)
            sp.wait_ge(stored, 16)

        def gather_value(i, more):
            each = 16 * 2 * CH
            return (i // 2 + more) * each if isinstance(i, int) else i[0] * each + more * each

        @block.gpsimd
        def _(pool):
            def gather(i):
                n = parity(i)
                col = i * (2 * CH) if isinstance(i, int) else i[0] * (4 * CH) + i[1] * 2 * CH
                await_(pool, emb_scaled, count(i, 1, 1, 0))
                await_(pool, gathered[n], gather_value(i, 0))
                pool.tensor_copy(rows_id[n][:], ids_all[:, bass.ds(col, 2 * CH)]).then_inc(slot_ids, 1)
                pool.wait_ge(slot_ids, count(i, 0, 1, 1))
                pool.tensor_tensor(wait_carrier[:], off_sb[:, 0:1], off_sb[:, 0:1], ALU.add)
                for k in range(CH):
                    for h in range(2):
                        pool.indirect_dma_start(
                            emb[n][:, k, h, :], None, table[:, :],
                            bass.IndirectOffsetOnAxis(ap=rows_id[n][:, 2 * k + h:2 * k + h + 1], axis=0),
                        ).then_inc(gathered[n], 16)

            pool.wait_ge(s_ids_ready, 1)
            gather(0)
            gather(1)
            with pool.Fori(1, TILES // 2) as pair:
                gather((pair, 0))
                gather((pair, 1))

        @block.tensor
        def _(pe):
            pe.wait_ge(s_small, 16 * len(SMALL))
            pe.wait_ge(s_ws_ready, 1)
            pe.transpose(bank[0][:, 0:P], ws_sb[:], identity[:]).then_inc(s_wse_ps, 1)
            pe.wait_ge(s_wse, 1)
            pe.matmul(bank[1][:, 0:P], ws_e[:], ws_e[:], start=True, stop=True).then_inc(s_gram_ps, 1)
            pe.wait_ge(s_wsi_ready, 1)
            pe.matmul(bank[2][0:1, 0:PR], owner_sb[:, 0, 0:1], wsi_sb[:, 0, :], start=True,
                      stop=True).then_inc(s_wsum_ps, 1)
            pe.wait_ge(s_w1, 32)
            for m in range(KH1):
                for k in range(KO):
                    mm = pe.matmul(bank[3][:, m:m + 1], w1_sb[:, k, m * P:(m + 1) * P], bl_sb[:, k:k + 1],
                                   start=(k == 0), stop=(k == KO - 1))
            mm.then_inc(s_b1_ps, 1)
            pe.wait_ge(s_mix_ready, 1)
            for k in range(QK + 1):
                mm = pe.matmul(bank[4][:], mix_w[:, k, :], wl_sb[:, k, :], start=(k == 0),
                               stop=(k == QK))
            mm.then_inc(s_mix_ps, 1)
            pe.wait_ge(s_gramw, 2)
            pe.wait_ge(s_fold_ready, 1)
            pe.wait_ge(s_bias, 96)
            pe.wait_ge(s_wd_ready, 1)
            pe.wait_ge(s_const, 1)

            def turn(i):
                n = parity(i)
                pe.wait_ge(gathered[n], gather_value(i, 1))
                for g, chunks in enumerate(GROUPS):
                    if g < 2:
                        await_(pe, prod_done, count(i, 0, NG, g - 1))
                        if g == 1:
                            await_(pe, x_done, count(i, 0, 1, 0))
                    else:
                        pe.wait_ge(turned_out, count(i, 0, NG, g - 1))
                    for c, k in enumerate(chunks):
                        mm = pe.transpose(feat_bank[g % 2][:, c * P:(c + 1) * P],
                                          emb[n][:, k, :, :].rearrange("p h d -> p (h d)"), identity[:])
                    if g == NG - 1:
                        pe.wait_ge(dense_got[n], (i // 2 + 1) * 16 if isinstance(i, int) else i[0] * 16 + 16)
                        for k in range(KD):
                            mm = pe.matmul(feat_bank[1][:, P:2 * P], dense_in[n][:, k, :], wd_sb[:, k, :],
                                           start=(k == 0), stop=(k == KD - 1))
                    mm.then_inc(turned, 1)

            def g_product(i, g):
                pe.wait_ge(turned_out, count(i, 0, NG, min(g + 3, NG)))
                if g == 1:
                    pe.wait_ge(x_scaled, count(i, 0, 1, 1))
                if g >= 2:
                    pe.wait_ge(prod_done, count(i, 0, NG, g - 1))
                for c, k in enumerate(GROUPS[g]):
                    mm = pe.matmul(feat_bank[g % 2][:, c * P:(c + 1) * P], emb_t[:, k, :], gram_w[:],
                                   start=True, stop=True)
                if g == NG - 1:
                    mm = pe.transpose(feat_bank[1][:, P:2 * P], x_n[:], identity[:])
                mm.then_inc(g_done, 1)

            def fold(i, t, m):
                if m == 0:
                    pe.wait_ge(emb_scaled, count(i, 1, 1, 1))
                if m < 2:
                    await_(pe, h1_out if m == 0 else yv_out, count(i, 3, 1, 1) + 0)
                    if m == 1:
                        await_(pe, h2_out, count(i, 3, 1, 1))
                else:
                    pe.wait_ge(fold_out, count(i, 1, NF, m - 1))
                for n, (k, s, width) in enumerate(FOLDS[m]):
                    c, s0 = s - m * BS, s - samples_of(k)[0]
                    mm = pe.matmul(fold_bank[m % 2][:, c * PR:(c + width) * PR],
                                   emb_n[:, k, :, :].rearrange("p h d -> p (h d)"),
                                   fold_w[:, k, s0:s0 + width, :].rearrange("p s q -> p (s q)"),
                                   start=(n == 0), stop=(n == len(FOLDS[m]) - 1), skip_group_check=True)
                mm.then_inc(fold_done, 1)

            def project(i, s):
                h, m = divmod(s, NF)
                pe.wait_ge(fold_out, count(i, 1, NF, m + 1))
                await_(pe, norm_done, count(i, 1, BLOCKS, s - 1))
                y = y_bank[s % 2][:]
                pe.matmul(y, wg_hi[:], folded[:, h, m, :], start=True, stop=False)
                pe.matmul(y, wg_lo[:], folded[0:D, h, m, :], start=False, stop=False)
                pe.matmul(y, bias_w[:], bias_m[:], start=False, stop=True).then_inc(y_done, 1)

            def gram(i, s):
                n, u = parity(i) ^ 1, s // 2
                pe.wait_ge(norm_done, count(i, 1, BLOCKS, s + 1))
                if s == 0:
                    pe.wait_ge(x_done, count(i, 1, 1, 1))
                if s % 2 == 0:
                    await_(pe, gram_out, count(i, 1, 4, u - 1))
                for b in range(s * BS, (s + 1) * BS):
                    g, j = divmod(b, 4)
                    c = (g - 2 * u * BS // 4) * TC
                    mm = pe.matmul(gram_bank[u % 2][32 * j:32 * j + 32, c:c + TC], tt[n][:, b, 0:PR],
                                   tt[n][:, b, :], start=True, stop=True)
                if s == BLOCKS - 1:
                    for j in range(4):
                        mm = pe.matmul(gram_bank[1][32 * j:32 * j + 32, 384:384 + GR], ones[:],
                                       tt[n][:, j::4, PR], start=True, stop=True)
                mm.then_inc(gram_done, 1)

            def interact(i, ks, last_fold):
                if ks[0] == 0:
                    pe.wait_ge(regrouped, count(i, 2, 256, 256))
                    if last_fold:
                        pe.wait_ge(fold_out, count(i, 1, NF, NF - 1))
                for k in ks:
                    mm = pe.matmul(fold_bank[0][:], pairs[:, :, :, k].rearrange("p j g -> p (j g)"),
                                   wl_sb[:, k, :], start=(k == 0), stop=(k == QK))
                if ks[-1] == QK:
                    mm.then_inc(z_done, 1)

            def turn_z(i, last_fold):
                pe.wait_ge(z_scaled, count(i, 2, 1, 1))
                if last_fold:
                    pe.wait_ge(fold_out, count(i, 1, NF, NF))
                for k in range(KO):
                    mm = pe.transpose(fold_bank[1][:, k * P:(k + 1) * P], z_n[:, k * P:(k + 1) * P], identity[:])
                mm.then_inc(zt_done, 1)

            def hidden1(i):
                first = (i - 2) * P if isinstance(i, int) else pe.snap(i[0] * (2 * P) + (i[1] - 2) * P)
                pe.wait_ge(zt_out, count(i, 2, 1, 1))
                for m in range(KH1):
                    for k in range(KO + KD):
                        if k < KO:
                            rhs = z_t[:, k, :]
                        else:
                            rhs = dense_all[:, k - KO, bass.ds(first, P)].rearrange("p (g j) -> p j g", j=4)
                        mm = pe.matmul(fold_bank[0][:, m * P:(m + 1) * P], w1_sb[:, k, m * P:(m + 1) * P], rhs,
                                       start=(k == 0), stop=(k == KO + KD - 1))
                mm.then_inc(h1_done, 1)

            def hidden2(i):
                pe.wait_ge(h1_out, count(i, 2, 1, 1))
                for m in range(KH2):
                    for k in range(KH1):
                        mm = pe.matmul(fold_bank[1][:, m * P:(m + 1) * P], w2_sb[:, k, m * P:(m + 1) * P],
                                       h1_t[:, k, :], start=(k == 0), stop=(k == KH1 - 1))
                mm.then_inc(h2_done, 1)

            def last_layer(i):
                pe.wait_ge(h2_out, count(i, 2, 1, 1))
                for k in range(KH2):
                    mm = pe.matmul(fold_bank[1][0:1, H2:H2 + P], w3_sb[:, k:k + 1], h2_t[:, k, :],
                                   start=(k == 0), stop=(k == KH2 - 1))
                mm.then_inc(yv_done, 1)

            ready = []

            def step(i, a, c, t):
                if c:
                    for m in range(NF):
                        fold(i, t, m)
                if a:
                    turn(i)
                if t and not ready:
                    pe.wait_ge(s_wl_ready, 1)
                    pe.wait_ge(s_w1_ready, 1)
                    pe.wait_ge(s_dense, 16)
                    ready.append(True)
                for s in range(BLOCKS + 2):
                    if c and s < BLOCKS:
                        project(i, s)
                    if a and 1 <= s <= NG:
                        g_product(i, s - 1)
                    if t and 2 <= s <= 3:
                        interact(i, range(0, 3) if s == 2 else range(3, QK + 1), c)
                    if c and s >= 2:
                        gram(i, s - 2)
                    if t and s == 6:
                        turn_z(i, c)
                    if t and s == 7:
                        hidden1(i)
                    if t and s == 8:
                        hidden2(i)
                    if t and s == 9:
                        last_layer(i)

            run_steps(pe, step)

        @block.scalar
        def _(act):
            act.wait_ge(s_wse_ps, 1)
            act.activation(ws_e[:], bank[0][:, 0:P], ACT.Copy).then_inc(s_wse, 1)
            act.wait_ge(s_gram_ps, 1)
            act.wait_ge(s_const, 1)
            for h in range(2):
                s = slice(h * D, (h + 1) * D)
                act.activation(gram_w[s, s], bank[1][s, s], ACT.Copy, scale=1.0 / E).then_inc(s_gramw, 1)

            def sqrt(dst, src, scale, done):
                act.activation(dst, src, ACT.Sqrt, bias=eps[:], scale=scale).then_inc(done, 1)

            def turn_out(i):
                await_(act, g_done, count(i, 0, NG, 0))
                for g, chunks in enumerate(GROUPS):
                    act.wait_ge(turned, count(i, 0, NG, g + 1))
                    n = len(chunks)
                    act.activation(emb_t[:, chunks[0]:chunks[0] + n, :].rearrange("p k r -> p (k r)"),
                                   feat_bank[g % 2][:, 0:n * P], ACT.Copy).then_inc(turned_out, 1)
                act.activation(junk_x[:], feat_bank[1][:, P:2 * P], ACT.Square, accum_out=var_x[:]).then_inc(x_sq, 1)
                act.wait_ge(x_sq, count(i, 0, 1, 1))
                sqrt(std_x[:], var_x[:], 1.0 / E, x_std)

            def gram_copy(i, u):
                act.wait_ge(gram_done, count(i, 1, BLOCKS, 2 * u + 2))
                if u == 0:
                    await_(act, regrouped, count(i, 1, 256, 0))
                g = GR // 4
                if u == 3:
                    act.activation(gram_s[:, 2, :, QK], gram_bank[1][:, 384:384 + GR], ACT.Copy)
                src = gram_bank[u % 2][:, 0:g * TC].rearrange("p (g q) -> p g q", q=TC)
                dst = gram_s[:, :, u * g:(u + 1) * g, :]
                act.activation(dst[:, :, :, 0:QK].rearrange("p r g k -> p g k r"),
                               src[:, :, 0:SL].rearrange("p g (k r) -> p g k r", r=4), ACT.Copy)
                act.activation(dst[:, 0:2, :, QK].rearrange("p r g -> p g r"), src[:, :, PR:TC],
                               ACT.Copy).then_inc(gram_low, 1)

            def step(i, a, c, t):
                if c:
                    await_(act, y_done, count(i, 1, BLOCKS, 0))
                    for m in range(NF):
                        act.wait_ge(fold_done, count(i, 1, NF, m + 1))
                        for h in range(2):
                            act.activation(folded[0:D, h, m, :], fold_bank[m % 2][h * D:(h + 1) * D, :],
                                           ACT.Copy).then_inc(fold_high, 1)
                if a:
                    turn_out(i)
                for s in range(BLOCKS + 2):
                    if c and s < BLOCKS:
                        act.wait_ge(y_done, count(i, 1, BLOCKS, s + 1))
                        await_(act, var_done, count(i, 1, BLOCKS, s - 1))
                        act.activation(square[s % 2][:].rearrange("p s q -> p (s q)"), y_bank[s % 2][:],
                                       ACT.Square).then_inc(sq_done, 1)
                    if a and s == 6:
                        act.wait_ge(var1_done, count(i, 0, 1, 1))
                        sqrt(std1[:], var1[:], 1.0, std1_done)
                    if c and s < BLOCKS:
                        act.wait_ge(var_done, count(i, 1, BLOCKS, s + 1))
                        sqrt(std2[s % 2][:], var2[s % 2][:], 1.0 / PR, std_done)
                    if a and s == 1:
                        act.wait_ge(x_rstd, count(i, 0, 1, 1))
                        act.activation(x_n[:], feat_bank[1][:, P:2 * P], ACT.Copy,
                                       scale=rstd_x[:]).then_inc(x_scaled, 1)
                    if c and s in (4, 6, 8, 9):
                        gram_copy(i, (4, 6, 8, 9).index(s))
                    if t and s == 4:
                        act.wait_ge(z_done, count(i, 2, 1, 1))
                        act.activation(junk_z[:], fold_bank[0][:], ACT.Square, accum_out=var3[:]).then_inc(z_sq, 1)
                        act.wait_ge(z_sq, count(i, 2, 1, 1))
                        sqrt(std3[:], var3[:], 1.0 / O, z_std)
                    if t and s == 5:
                        act.wait_ge(z_rstd, count(i, 2, 1, 1))
                        act.activation(z_n[:], fold_bank[0][:, 0:OU], ACT.Copy, scale=rstd3[:]).then_inc(z_scaled, 1)
                    if t and s == 6:
                        act.wait_ge(zt_done, count(i, 2, 1, 1))
                        act.activation(z_t[:].rearrange("p k b -> p (k b)"), fold_bank[1][:, 0:OU],
                                       ACT.Copy).then_inc(zt_out, 1)
                    if t and s == 7:
                        act.wait_ge(h1_done, count(i, 2, 1, 1))
                        for m in range(KH1):
                            ins = act.activation(h1_t[:, m, :], fold_bank[0][:, m * P:(m + 1) * P], ACT.Relu,
                                                 bias=b1_sb[:, m:m + 1])
                        ins.then_inc(h1_out, 1)
                    if t and s == 8:
                        act.wait_ge(h2_done, count(i, 2, 1, 1))
                        for m in range(KH2):
                            ins = act.activation(h2_t[:, m, :], fold_bank[1][:, m * P:(m + 1) * P], ACT.Relu,
                                                 bias=b2_sb[:, m:m + 1])
                        ins.then_inc(h2_out, 1)
                    if t and s == 9:
                        first = (i - 2) * P if isinstance(i, int) else act.snap(i[0] * (2 * P) + (i[1] - 2) * P)
                        act.wait_ge(yv_done, count(i, 2, 1, 1))
                        act.activation(y_all[0:1, bass.ds(first, P)].rearrange("o (g j) -> o j g", j=4),
                                       fold_bank[1][0:1, H2:H2 + P].rearrange("o (j g) -> o j g", j=4),
                                       ACT.Copy).then_inc(yv_out, 1)

            run_steps(act, step)

        @block.vector
        def _(dve):
            done = [0]

            def link(ins):
                done[0] += 1
                ins.then_inc(s_prep, 1)
                dve.wait_ge(s_prep, done[0])

            def centre(w, mean, width):
                link(dve.tensor_reduce(mean, w, AX.X, ALU.add))
                link(dve.tensor_scalar(mean, mean, 1.0 / width, None, ALU.mult))
                link(dve.tensor_tensor(w, w, mean.unsqueeze(2).broadcast_to(list(w.shape)), ALU.subtract))

            dve.wait_ge(s_ids, 32)
            dve.tensor_tensor(ids_all[:].rearrange("p (t c) -> p t c", c=2 * CH),
                              ids_all[:].rearrange("p (t c) -> p t c", c=2 * CH),
                              off_sb[:].unsqueeze(1).broadcast_to([P, TILES, 2 * CH]),
                              ALU.add).then_inc(s_ids_ready, 1)
            dve.memset(eps[:], EPS)
            dve.memset(ones[:], 1.0)
            dve.memset(tt[0][:, :, PR + 1:TC], 1.0)
            dve.memset(tt[1][:, :, PR + 1:TC], 1.0)
            dve.memset(gram_s[:, 3, :, QK], 1.0)
            link(dve.memset(mix_w[:], 0.0))
            dve.memset(gram_w[:], 0.0).then_inc(s_const, 1)
            dve.wait_ge(s_ws, 16 * len(WS))
            centre(ws_sb[:].unsqueeze(1), mean_a[:], E)
            dve.tensor_tensor(wg_sb[:], ws_sb[:], gs_sb[:], ALU.mult).then_inc(s_ws_ready, 1)
            dve.wait_ge(s_wsi, 16 * len(WSI))
            centre(wsi_sb[:], mean_b[:], PR)
            dve.tensor_scalar(mean_a[:], mean_a[:], 1.0, None, ALU.mult).then_inc(s_wsi_ready, 1)
            dve.tensor_tensor(fold_w[:], wsi_sb[:].unsqueeze(2).broadcast_to([P, CH, SPAN, PR]),
                              owner_sb[:].unsqueeze(3).broadcast_to([P, CH, SPAN, PR]),
                              ALU.mult).then_inc(s_fold_ready, 1)
            centre(wd_sb[:], mean_c[:], E)
            dve.tensor_scalar(mean_a[:], mean_a[:], 1.0, None, ALU.mult).then_inc(s_wd_ready, 1)
            dve.wait_ge(s_wsum_ps, 1)
            link(dve.tensor_copy(wsum_row[:], bank[2][0:1, 0:PR].unsqueeze(1).broadcast_to([1, BS, PR])))
            wsum = wsum_row[:].rearrange("o s q -> o (s q)")
            dve.tensor_copy(bs_parts[:, 0, :], bs_row[:])
            dve.tensor_copy(wg_hi[:], wg_sb[:])
            link(dve.tensor_copy(wsum_parts[:, 0, :], wsum))
            dve.tensor_tensor(bs_parts[:, 1, :], bs_row[:], bs_parts[:, 0, :], ALU.subtract)
            dve.tensor_tensor(wg_lo[:], wg_sb[0:D, :], wg_hi[0:D, :], ALU.subtract)
            dve.tensor_tensor(wsum_parts[:, 1, :], wsum, wsum_parts[:, 0, :], ALU.subtract).then_inc(s_parts, 1)
            dve.wait_ge(s_small, 16 * len(SMALL))
            for dst, u, v in ((gg, gp, gq), (gb, gp, bq), (bg, bp, gq), (bb, bp, bq)):
                link(dve.tensor_scalar(dst[:], v[:], u[:], None, ALU.mult))
            link(dve.tensor_scalar(mix_w[:, 0:QK, 96], bb[:], float(E), None, ALU.mult))
            link(dve.tensor_copy(mix_w[:, QK, 64:65], bp[:]))
            for k in range(QK):
                link(dve.tensor_scalar(mix_w[:, k, PR:2 * PR], eye_p_sb[:], gb[:, k:k + 1], None, ALU.mult))
                link(dve.scalar_tensor_tensor(out=mix_w[:, k, PR:2 * PR], in0=eye_q_sb[:, k, :],
                                              scalar=bg[:, k:k + 1], in1=mix_w[:, k, PR:2 * PR],
                                              op0=ALU.mult, op1=ALU.add))
            dve.wait_ge(s_wl, 16)
            centre(wl_sb[:], mean_d[:], O)
            dve.tensor_scalar(mean_a[:], mean_a[:], 1.0, None, ALU.mult).then_inc(s_mix_ready, 1)
            dve.wait_ge(s_mix_ps, 1)
            for k in range(QK):
                dve.tensor_scalar(wl_sb[:, k, :], wl_sb[:, k, :], gg[:, k:k + 1], None, ALU.mult)
            dve.tensor_scalar(wl_sb[0:PR, QK, :], wl_sb[0:PR, QK, :], gp[0:PR, :], None, ALU.mult)
            for r in (1, 2):
                dve.tensor_copy(wl_sb[r * PR:(r + 1) * PR, QK, :], bank[4][r * PR:(r + 1) * PR, :])
            dve.tensor_copy(wl_sb[3 * PR:P, QK, :], bank[4][3 * PR:P, :]).then_inc(s_wl_ready, 1)
            dve.wait_ge(s_b1_ps, 1)
            for k in range(KO):
                dve.tensor_scalar(w1_sb[:, k, :], w1_sb[:, k, :], gl_sb[:, k:k + 1], None, ALU.mult)
            dve.tensor_tensor(b1_sb[:], b1_sb[:], bank[3][:, 0:KH1], ALU.add).then_inc(s_w1_ready, 1)

            def products(i, g):
                chunks = GROUPS[g]
                dve.wait_ge(g_done, count(i, 0, NG, g + 1))
                sl = slice(chunks[0], chunks[-1] + 1)
                dve.tensor_tensor(prod[:, sl, :, :].rearrange("p k h d -> p (k h d)"),
                                  feat_bank[g % 2][:, 0:len(chunks) * P],
                                  emb[parity(i)][:, sl, :, :].rearrange("p k h d -> p (k h d)"),
                                  ALU.mult).then_inc(prod_done, 1)

            def gram_pick(i, u):
                dve.wait_ge(gram_low, count(i, 1, 4, u + 1))
                dve.tensor_copy(wait_carrier_v[:, u:u + 1], eps[:])
                g = GR // 4
                src = gram_bank[u % 2][:, 0:g * TC].rearrange("p (g q) -> p g q", q=TC)
                dve.copy_predicated(
                    gram_s[:, :, u * g:(u + 1) * g, 0:QK].rearrange("p r g k -> p g k r"),
                    take_upper[:].rearrange("p (k r) -> p k r", r=4).unsqueeze(1).broadcast_to([P, g, QK, 4]),
                    src[:, :, SL:PR].rearrange("p g (k r) -> p g k r", r=4)).then_inc(gram_out, 1)

            def step(i, a, c, t):
                if c:
                    for m in range(NF):
                        dve.wait_ge(fold_high, count(i, 1, 2 * NF, 2 * m + 2))
                        for h in range(2):
                            low = dve.tensor_tensor(folded[D:P, h, m, :], fold_bank[m % 2][h * D:(h + 1) * D, :],
                                                    folded[0:D, h, m, :], ALU.subtract)
                        low.then_inc(fold_out, 1)
                if a:
                    dve.wait_ge(x_std, count(i, 0, 1, 1))
                    dve.reciprocal(rstd_x[:], std_x[:]).then_inc(x_rstd, 1)
                for s in range(BLOCKS):
                    if c:
                        dve.wait_ge(sq_done, count(i, 1, BLOCKS, s + 1))
                        dve.tensor_reduce(var2[s % 2][:], square[s % 2][:], AX.X, ALU.add).then_inc(var_done, 1)
                    if a and 1 <= s <= NG:
                        products(i, s - 1)
                    if a and s == NG:
                        dve.tensor_scalar(tt[parity(i)][:, :, PR], feat_bank[1][:, P:2 * P], gd_sb[:], bd_sb[:],
                                          ALU.mult, ALU.add).then_inc(x_done, 1)
                    if c and s in (5, 7):
                        gram_pick(i, (5, 7).index(s))
                    if a and s == 5:
                        dve.wait_ge(prod_done, count(i, 0, NG, NG))
                        dve.tensor_reduce(var1[:], prod[:], AX.X, ALU.add).then_inc(var1_done, 1)
                    if a and s == 6:
                        dve.wait_ge(std1_done, count(i, 0, 1, 1))
                        dve.reciprocal(rstd1[:], std1[:]).then_inc(rstd1_done, 1)
                    if c:
                        dve.wait_ge(std_done, count(i, 1, BLOCKS, s + 1))
                        dve.reciprocal(rstd2[s % 2][:], std2[s % 2][:]).then_inc(rstd_done, 1)
                        dve.wait_ge(rstd_done, count(i, 1, BLOCKS, s + 1))
                        dve.tensor_tensor(tt[parity(i) ^ 1][:, s * BS:(s + 1) * BS, 0:PR],
                                          y_bank[s % 2][:].rearrange("p (s q) -> p s q", q=PR),
                                          rstd2[s % 2][:].unsqueeze(2).broadcast_to([P, BS, PR]),
                                          ALU.mult).then_inc(norm_done, 1)
                    if a and s == 6:
                        dve.wait_ge(rstd1_done, count(i, 0, 1, 1))
                        await_(dve, fold_done, count(i, 0, NF, 0))
                        dve.tensor_tensor(emb_n[:], emb[parity(i)][:],
                                          rstd1[:].unsqueeze(3).broadcast_to([P, CH, 2, D]),
                                          ALU.mult).then_inc(emb_scaled, 1)
                    if t and s == 4:
                        dve.wait_ge(z_std, count(i, 2, 1, 1))
                        dve.reciprocal(rstd3[:], std3[:]).then_inc(z_rstd, 1)
                if c:
                    gram_pick(i, 2)
                    gram_pick(i, 3)

            run_steps(dve, step)


def kernel(**inputs):
    from concourse import bacc
    from concourse.bass_utils import run_bass_kernel_spmd

    a = {k: np.asarray(v) for k, v in inputs.items()}
    row = np.arange(CH * P).reshape(CH, P)
    feat = (row % NS).T
    owner = (row // NS).T - (np.arange(CH) * P // NS)[None, :]
    base = np.concatenate([[0], np.cumsum(VOCAB)[:-1]])
    by_chunk = a["ids"].astype(np.int32, copy=False).reshape(TILES, 2, CH, P).transpose(3, 0, 2, 1)
    offsets = np.repeat(base[feat][:, :, None], 2, axis=2).reshape(P, 2 * CH)

    pr = np.arange(P)[:, None] % PR
    slot = 4 * np.arange(QK)[None, :] + (np.arange(P) // PR)[:, None]
    far = (pr % SL < slot) == (pr >= SL)
    q = slot + SL * far
    wl_t = a["L0_rec_Wl"].T
    wl = np.zeros((P, QK + 1, O), wl_t.dtype)
    hi, lo = np.maximum(pr, q) + 1, np.minimum(pr, q) + 1
    rr, kk = np.nonzero((pr % SL != slot) | (pr < SL))
    wl[rr, kk] = wl_t[(hi * (hi - 1) // 2 + lo)[rr, kk]]
    row_p, all_slots = np.arange(P)[:, None] % PR, np.arange(SL)[None, :]
    upper = (row_p % SL < all_slots) == (row_p >= SL)
    pr = pr[:, 0]
    first = np.arange(1, PR + 1)
    wl[0:PR, QK] = wl_t[first * (first - 1) // 2]

    def cols(v, n):
        return v.reshape(n, P).T

    f = np.float32
    args = {
        "table": np.concatenate([a[f"tbl_{n}"] for n in range(NS)]),
        "ids": by_chunk.reshape(P, TILES * 2 * CH),
        "offsets": offsets.astype(np.int32),
        "dense_t": a["r_dense_t"].T,
        "ident": np.eye(P, dtype=f),
        "ws_t": np.concatenate([a["L0_rec_Ws"].T] * 2),
        "gs": np.broadcast_to(a["L0_rec_gs"], (P, E)),
        "bs": a["L0_rec_bs"][None],
        "wsi": a["L0_rec_Wsi"].T[feat],
        "owner": (owner[:, :, None] == np.arange(SPAN)).astype(f),
        "wd_t": a["L0_rec_Wd"].T.reshape(KD, P, E).transpose(1, 0, 2),
        "gd": a["L0_rec_gd"][:, None], "bd": a["L0_rec_bd"][:, None],
        "wl": wl,
        "gsi_p": a["L0_rec_gsi"][pr][:, None], "gsi_q": a["L0_rec_gsi"][q],
        "bsi_p": a["L0_rec_bsi"][pr][:, None], "bsi_q": a["L0_rec_bsi"][q],
        "eye_p": (pr[:, None] == np.arange(PR)).astype(f),
        "eye_q": (q[:, :, None] == np.arange(PR)).astype(f),
        "w1": np.concatenate([a["W_top1"][:OU], a["W_top1"][O:]]).reshape(KO + KD, P, H1).transpose(1, 0, 2),
        "gl": cols(a["L0_rec_gl"][:OU], KO), "bl": cols(a["L0_rec_bl"][:OU], KO),
        "b1": cols(a["b_top1"], KH1),
        "w2": a["W_top2"].reshape(KH1, P, H2).transpose(1, 0, 2),
        "b2": cols(a["b_top2"], KH2),
        "upper": upper.astype(np.int32),
        "w3": a["W_top3"].reshape(KH2, P).T,
    }
    nc = bacc.Bacc("TRN2", target_bir_lowering=False, num_devices=1)
    args = {k: np.ascontiguousarray(v) for k, v in args.items()}
    aps = {k: nc.dram_tensor(f"in_{k}", v.shape, mybir.dt.from_np(v.dtype), kind="ExternalInput").ap()
           for k, v in args.items()}
    out = nc.dram_tensor("out_y", (B, 1), F32, kind="ExternalOutput").ap()
    build_tower(nc, **aps, out=out)
    r = run_bass_kernel_spmd(nc, [{f"in_{k}": v for k, v in args.items()}], core_ids=[0])
    return r.results[0]["out_y"]
```

```python
from contextlib import ExitStack

import numpy as np

import concourse.bass as bass
from concourse import mybir

ALU = mybir.AluOpType
ACT = mybir.ActivationFunctionType
AX = mybir.AxisListType
F32 = mybir.dt.float32
I32 = mybir.dt.int32
F16 = mybir.dt.float16

P = 128
VOCAB = [12500, 125000, 12500, 1250, 12500, 125000, 125000, 1000, 12500, 12500, 1250, 1250, 1250,
         1250, 12500, 12500, 12500, 1250, 1250, 1000, 1000, 1000, 1000, 1000, 1000, 1000]
B = 2048
NS = len(VOCAB)
D = 64
DD = 256
E = 128
PR = 32
O = 512
OU = 384
H1, H2 = 512, 256
EPS = 1e-5

TILES = B // P
HALF = P // 2
CH = HALF * NS // P
SPAN = 6
BS = 16
BLOCKS = P // BS
GR = P // 4
SL = PR // 2
QK = SL // 4
TC = PR + 2
KD, KO, KH1, KH2 = DD // P, OU // P, H1 // P, H2 // P

GROUPS = [range(0, 4), range(4, 8), range(8, 12), range(12, 13)]
NG = len(GROUPS)


def samples_of(k):
    return k * P // NS, (k * P + P - 1) // NS


def fold_plan(m):
    plan = []
    for k in range(CH):
        a, b = samples_of(k)
        a, b = max(a, m * BS), min(b, m * BS + BS - 1)
        if a <= b:
            plan.append((k, a, b - a + 1))
    return plan


FOLDS = [fold_plan(m) for m in range(HALF // BS)]
NF = len(FOLDS)


def count(step, lag, per_tile, k):
    if isinstance(step, int):
        return (step - lag) * per_tile + k
    pair, odd = step
    return pair * (2 * per_tile) + ((odd - lag) * per_tile + k)


def await_(eng, sem, value):
    if isinstance(value, int) and value <= 0:
        return
    eng.wait_ge(sem, value)


def parity(step):
    return step % 2 if isinstance(step, int) else step[1]


def run_steps(eng, step_fn):
    for i in range(4):
        step_fn(i, True, i >= 1, i >= 2, i >= 3)
    with eng.Fori(2, TILES // 2) as pair:
        step_fn((pair, 0), True, True, True, True)
        step_fn((pair, 1), True, True, True, True)
    step_fn(TILES, False, True, True, True)
    step_fn(TILES + 1, False, False, True, True)
    step_fn(TILES + 2, False, False, False, True)


def build_tower(nc, table, ids, offsets, dense_t, ident, ws_t, gs, bs, wsi, owner, wd_t, gd, bd,
                wl, gsi_p, gsi_q, bsi_p, bsi_q, eye_p, eye_q, w1, gl, bl, b1, w2, b2, w3, upper, out):
    with ExitStack() as ctx:
        def sb(name, shape, dt=F32):
            return ctx.enter_context(nc.sbuf_tensor(name, shape, dt))

        def sem(name):
            return ctx.enter_context(nc.semaphore(name))

        bank = [ctx.enter_context(nc.psum_tensor(f"bank{n}", [P, 512], F32)) for n in range(8)]
        feat_bank = bank[0:2]
        fold_bank = bank[2]
        tower_bank = bank[3]
        y_bank = bank[4:6]
        gram_bank = bank[6:8]

        identity = sb("identity", [P, P])
        eps = sb("eps", [P, 1])
        ones = sb("ones", [P, PR])
        ids_all = sb("ids_all", [P, TILES * 2 * CH], I32)
        off_sb = sb("off_sb", [P, 2 * CH], I32)
        ws_sb = sb("ws_sb", [P, E])
        gs_sb = sb("gs_sb", [P, E])
        wg_sb = sb("wg_sb", [P, E])
        ws_e = sb("ws_e", [P, P])
        gram_w = sb("gram_w", [P, P])
        wg_hi, wg_lo = sb("wg_hi", [P, E], F16), sb("wg_lo", [D, E], F16)
        bs_row = sb("bs_row", [1, E])
        wsum_row = sb("wsum_row", [1, BS, PR])
        bs_parts = sb("bs_parts", [1, 2, E], F16)
        wsum_parts = sb("wsum_parts", [1, 2, BS * PR], F16)
        bias_w = sb("bias_w", [3, E], F16)
        bias_m = sb("bias_m", [3, BS * PR], F16)
        wsi_sb = sb("wsi_sb", [P, CH, PR])
        owner_sb = sb("owner_sb", [P, CH, SPAN])
        fold_w = sb("fold_w", [P, CH, SPAN, PR])
        wd_sb = sb("wd_sb", [P, KD, E])
        gd_sb, bd_sb = sb("gd_sb", [P, 1]), sb("bd_sb", [P, 1])
        wl_sb = sb("wl_sb", [P, QK + 1, O])
        gp, gq = sb("gp", [P, 1]), sb("gq", [P, QK])
        bp, bq = sb("bp", [P, 1]), sb("bq", [P, QK])
        gg, gb, bg, bb = (sb(n, [P, QK]) for n in ("gg", "gb", "bg", "bb"))
        eye_p_sb = sb("eye_p_sb", [P, PR])
        eye_q_sb = sb("eye_q_sb", [P, QK, PR])
        take_upper = sb("take_upper", [P, SL], I32)
        mix_w = sb("mix_w", [P, QK + 1, P])
        w1_sb = sb("w1_sb", [P, KO + KD, H1])
        gl_sb, bl_sb = sb("gl_sb", [P, KO]), sb("bl_sb", [P, KO])
        b1_sb, b2_sb = sb("b1_sb", [P, KH1]), sb("b2_sb", [P, KH2])
        w2_sb = sb("w2_sb", [P, KH1, H2])
        w3_sb = sb("w3_sb", [P, KH2])
        mean_a, mean_b = sb("mean_a", [P, 1]), sb("mean_b", [P, CH])
        mean_c, mean_d = sb("mean_c", [P, KD]), sb("mean_d", [P, QK + 1])
        dense_all = sb("dense_all", [P, KD, B])

        wait_carrier_v = sb("wait_carrier_v", [P, 4])
        wait_carrier = sb("wait_carrier", [P, 1], I32)
        rows_id = [sb(f"rows_id{n}", [P, 2 * CH], I32) for n in range(2)]
        emb = [sb(f"emb{n}", [P, CH, 2, D]) for n in range(2)]
        dense_in = [sb(f"dense_in{n}", [P, KD, P]) for n in range(2)]
        emb_t = sb("emb_t", [P, CH, P])
        prod = sb("prod", [P, CH, 2, D])
        var1, std1, rstd1 = (sb(n, [P, CH, 2]) for n in ("var1", "std1", "rstd1"))
        emb_n = sb("emb_n", [P, CH, 2, D])
        junk_x = sb("junk_x", [P, E])
        var_x, std_x, rstd_x = (sb(n, [P, 1]) for n in ("var_x", "std_x", "rstd_x"))
        x_n = sb("x_n", [P, E])
        folded = sb("folded", [P, 2, NF, BS * PR], F16)
        square = [sb(f"square{n}", [P, BS, PR]) for n in range(2)]
        var2 = [sb(f"var2_{n}", [P, BS]) for n in range(2)]
        std2 = [sb(f"std2_{n}", [P, BS]) for n in range(2)]
        rstd2 = [sb(f"rstd2_{n}", [P, BS]) for n in range(2)]
        tt = [sb(f"tt{n}", [P, P, TC]) for n in range(2)]
        gram_s = sb("gram_s", [P, 4, GR, QK + 1])
        pairs = sb("pairs", [P, 4, GR, QK + 1])
        junk_z = sb("junk_z", [P, O])
        var3, std3, rstd3 = (sb(n, [P, 1]) for n in ("var3", "std3", "rstd3"))
        z_n = sb("z_n", [P, OU])
        z_t = sb("z_t", [P, KO, P])
        h1_t = sb("h1_t", [P, KH1, P])
        h2_t = sb("h2_t", [P, KH2, P])
        y_all = sb("y_all", [1, B])

        s_ids, s_small, s_ws, s_wsi, s_wl, s_w1, s_dense = (
            sem(n) for n in ("ids_in", "small_in", "ws_in", "wsi_in", "wl_in", "w1_in", "dense_in_all"))
        dense_got = [sem(f"dense_got{n}") for n in range(2)]
        s_ids_ready, s_prep, s_ws_ready, s_wse_ps, s_wse, s_gram_ps, s_gramw = (
            sem(n) for n in ("ids_ready", "prep_step", "ws_ready", "wse_ps", "wse", "gramw_ps", "gramw"))
        s_wsi_ready, s_wsum_ps, s_fold_ready, s_wd_ready = (
            sem(n) for n in ("wsi_ready", "wsum_ps", "fold_ready", "wd_ready"))
        s_mix_ready, s_mix_ps, s_wl_ready, s_b1_ps, s_w1_ready, s_const, s_parts, s_bias = (
            sem(n) for n in ("mix_ready", "mix_ps", "wl_ready", "b1_ps", "w1_ready", "const_ready",
                             "parts_ready", "bias_rows_in"))
        slot_ids = sem("slot_ids")
        gathered = [sem(f"gathered{n}") for n in range(2)]
        turned, turned_out = sem("turned"), sem("turned_out")
        x_sq, x_std, x_rstd, x_scaled, x_done = (
            sem(n) for n in ("x_sq", "x_std", "x_rstd", "x_scaled", "x_done"))
        g_done, prod_done = sem("g_done"), sem("prod_done")
        var1_done, std1_done, rstd1_done, emb_scaled = (
            sem(n) for n in ("var1_done", "std1_done", "rstd1_done", "emb_scaled"))
        fold_done, fold_out = sem("fold_done"), sem("fold_out")
        fold_high = sem("fold_high")
        y_done, sq_done, var_done, std_done, rstd_done, norm_done, gram_done = (
            sem(n) for n in ("y_done", "sq_done", "var_done", "std_done", "rstd_done", "norm_done",
                             "gram_done"))
        gram_low, gram_out = sem("gram_low"), sem("gram_out")
        regrouped = sem("regrouped")
        z_done, z_sq, z_std, z_rstd, z_scaled, zt_done, zt_out = (
            sem(n) for n in ("z_done", "z_sq", "z_std", "z_rstd", "z_scaled", "zt_done", "zt_out"))
        h1_done, h1_out, h2_done, h2_out, yv_done, yv_out = (
            sem(n) for n in ("h1_done", "h1_out", "h2_done", "h2_out", "yv_done", "yv_out"))
        stored = sem("stored")

        SMALL = [(identity, ident), (gd_sb, gd), (bd_sb, bd), (gp, gsi_p), (gq, gsi_q), (bp, bsi_p),
                 (bq, bsi_q), (eye_p_sb, eye_p), (eye_q_sb, eye_q), (gl_sb, gl), (bl_sb, bl),
                 (b1_sb, b1), (b2_sb, b2), (w3_sb, w3), (take_upper, upper)]
        WS = [(ws_sb, ws_t), (gs_sb, gs), (bs_row, bs)]
        WSI = [(wsi_sb, wsi), (owner_sb, owner), (wd_sb, wd_t)]
        dense_tiles = dense_t.rearrange("(c k) b -> k c b", k=P)

        block = ctx.enter_context(nc.Block())

        @block.sync
        def _(sp):
            sp.dma_start(ids_all[:], ids[:, :]).then_inc(s_ids, 16)
            sp.dma_start(off_sb[:], offsets[:, :]).then_inc(s_ids, 16)
            for dst, src in WS:
                sp.dma_start(dst[:], src).then_inc(s_ws, 16)
            for dst, src in SMALL:
                sp.dma_start(dst[:], src).then_inc(s_small, 16)
            for dst, src in WSI:
                sp.dma_start(dst[:], src).then_inc(s_wsi, 16)
            sp.dma_start(dense_in[0][:], dense_tiles[:, :, 0:P]).then_inc(dense_got[0], 16)
            sp.dma_start(wl_sb[:], wl).then_inc(s_wl, 16)
            sp.dma_start(w1_sb[:], w1).then_inc(s_w1, 16)
            sp.dma_start(w2_sb[:], w2).then_inc(s_w1, 16)
            sp.dma_start(dense_all[:], dense_tiles).then_inc(s_dense, 16)

            sp.wait_ge(s_parts, 1)
            for row, (u, v) in enumerate([(0, 0), (0, 1), (1, 0)]):
                sp.dma_start(bias_w[row:row + 1, :], bs_parts[:, u, :]).then_inc(s_bias, 16)
                sp.dma_start(bias_m[row:row + 1, :], wsum_parts[:, v, :]).then_inc(s_bias, 16)

            def held(value):
                return value if isinstance(value, int) else sp.snap(value)

            def step(i, a, c, z, t):
                nxt = i + 1 if isinstance(i, int) else i[0] * 2 + (i[1] + 1)
                if not isinstance(i, int) or nxt < TILES:
                    first, free = held(nxt * P), held(count(i, 0, NG, 0))
                    await_(sp, turned, free)
                    dst = dense_in[1 - parity(i)]
                    sp.dma_start(dst[:], dense_tiles[:, :, bass.ds(first, P)]).then_inc(
                        dense_got[1 - parity(i)], 16)
                if z:
                    sp.wait_ge(gram_out, count(i, 2, 4, 4))
                    for j in range(4):
                        for r in range(4):
                            sp.dma_start(pairs[32 * r:32 * r + 32, j, :, :],
                                         gram_s[32 * j:32 * j + 32, r, :, :]).then_inc(regrouped, 16)

            for i in range(4):
                step(i, True, i >= 1, i >= 2, i >= 3)
            with sp.Fori(2, TILES // 2 - 1) as pair:
                step((pair, 0), True, True, True, True)
                step((pair, 1), True, True, True, True)
            step(TILES - 2, True, True, True, True)
            step(TILES - 1, True, True, True, True)
            step(TILES, False, True, True, True)
            step(TILES + 1, False, False, True, True)
            sp.wait_ge(yv_out, TILES)
            sp.dma_start(out.rearrange("n o -> o n"), y_all[:]).then_inc(stored, 16)
            sp.wait_ge(stored, 16)

        def gather_value(i, more):
            each = 16 * 2 * CH
            return (i // 2 + more) * each if isinstance(i, int) else i[0] * each + more * each

        @block.gpsimd
        def _(pool):
            def gather(i):
                n = parity(i)
                col = i * (2 * CH) if isinstance(i, int) else i[0] * (4 * CH) + i[1] * 2 * CH
                await_(pool, emb_scaled, count(i, 1, 1, 0))
                await_(pool, gathered[n], gather_value(i, 0))
                pool.tensor_copy(rows_id[n][:], ids_all[:, bass.ds(col, 2 * CH)]).then_inc(slot_ids, 1)
                pool.wait_ge(slot_ids, count(i, 0, 1, 1))
                pool.tensor_tensor(wait_carrier[:], off_sb[:, 0:1], off_sb[:, 0:1], ALU.add)
                for k in range(CH):
                    for h in range(2):
                        pool.indirect_dma_start(
                            emb[n][:, k, h, :], None, table[:, :],
                            bass.IndirectOffsetOnAxis(ap=rows_id[n][:, 2 * k + h:2 * k + h + 1], axis=0),
                        ).then_inc(gathered[n], 16)

            pool.wait_ge(s_ids_ready, 1)
            gather(0)
            gather(1)
            with pool.Fori(1, TILES // 2) as pair:
                gather((pair, 0))
                gather((pair, 1))

        @block.tensor
        def _(pe):
            pe.wait_ge(s_small, 16 * len(SMALL))
            pe.wait_ge(s_ws_ready, 1)
            pe.transpose(bank[0][:, 0:P], ws_sb[:], identity[:]).then_inc(s_wse_ps, 1)
            pe.wait_ge(s_wse, 1)
            pe.matmul(bank[1][:, 0:P], ws_e[:], ws_e[:], start=True, stop=True).then_inc(s_gram_ps, 1)
            pe.wait_ge(s_wsi_ready, 1)
            pe.matmul(bank[2][0:1, 0:PR], owner_sb[:, 0, 0:1], wsi_sb[:, 0, :], start=True,
                      stop=True).then_inc(s_wsum_ps, 1)
            pe.wait_ge(s_w1, 32)
            for m in range(KH1):
                for k in range(KO):
                    mm = pe.matmul(bank[3][:, m:m + 1], w1_sb[:, k, m * P:(m + 1) * P], bl_sb[:, k:k + 1],
                                   start=(k == 0), stop=(k == KO - 1))
            mm.then_inc(s_b1_ps, 1)
            pe.wait_ge(s_mix_ready, 1)
            for k in range(QK + 1):
                mm = pe.matmul(bank[4][:], mix_w[:, k, :], wl_sb[:, k, :], start=(k == 0),
                               stop=(k == QK))
            mm.then_inc(s_mix_ps, 1)
            pe.wait_ge(s_gramw, 2)
            pe.wait_ge(s_fold_ready, 1)
            pe.wait_ge(s_bias, 96)
            pe.wait_ge(s_wd_ready, 1)
            pe.wait_ge(s_const, 1)

            def turn(i, groups):
                n = parity(i)
                if groups[0] == 0:
                    pe.wait_ge(gathered[n], gather_value(i, 1))
                for g in groups:
                    chunks = GROUPS[g]
                    if g < 2:
                        await_(pe, prod_done, count(i, 0, NG, g - 1))
                        if g == 1:
                            await_(pe, x_done, count(i, 0, 1, 0))
                    else:
                        pe.wait_ge(turned_out, count(i, 0, NG, g - 1))
                    for c, k in enumerate(chunks):
                        mm = pe.transpose(feat_bank[g % 2][:, c * P:(c + 1) * P],
                                          emb[n][:, k, :, :].rearrange("p h d -> p (h d)"), identity[:])
                    if g == NG - 1:
                        pe.wait_ge(dense_got[n], (i // 2 + 1) * 16 if isinstance(i, int) else i[0] * 16 + 16)
                        for k in range(KD):
                            mm = pe.matmul(feat_bank[1][:, P:2 * P], dense_in[n][:, k, :], wd_sb[:, k, :],
                                           start=(k == 0), stop=(k == KD - 1))
                    mm.then_inc(turned, 1)

            def g_product(i, g):
                pe.wait_ge(turned_out, count(i, 0, NG, min(g + 3, NG)))
                if g == 1:
                    pe.wait_ge(x_scaled, count(i, 0, 1, 1))
                if g >= 2:
                    pe.wait_ge(prod_done, count(i, 0, NG, g - 1))
                for c, k in enumerate(GROUPS[g]):
                    mm = pe.matmul(feat_bank[g % 2][:, c * P:(c + 1) * P], emb_t[:, k, :], gram_w[:],
                                   start=True, stop=True)
                if g == NG - 1:
                    mm = pe.transpose(feat_bank[1][:, P:2 * P], x_n[:], identity[:])
                mm.then_inc(g_done, 1)

            def fold(i, m):
                if m == 0:
                    pe.wait_ge(emb_scaled, count(i, 1, 1, 1))
                await_(pe, fold_out, count(i, 1, NF, m))
                for n, (k, s, width) in enumerate(FOLDS[m]):
                    c, s0 = s - m * BS, s - samples_of(k)[0]
                    mm = pe.matmul(fold_bank[:, c * PR:(c + width) * PR],
                                   emb_n[:, k, :, :].rearrange("p h d -> p (h d)"),
                                   fold_w[:, k, s0:s0 + width, :].rearrange("p s q -> p (s q)"),
                                   start=(n == 0), stop=(n == len(FOLDS[m]) - 1), skip_group_check=True)
                mm.then_inc(fold_done, 1)

            def project(i, s):
                m, h = divmod(s, 2)
                pe.wait_ge(fold_out, count(i, 1, NF, m + 1))
                await_(pe, norm_done, count(i, 1, BLOCKS, s - 1))
                y = y_bank[s % 2][:]
                pe.matmul(y, wg_hi[:], folded[:, h, m, :], start=True, stop=False)
                pe.matmul(y, wg_lo[:], folded[0:D, h, m, :], start=False, stop=False)
                pe.matmul(y, bias_w[:], bias_m[:], start=False, stop=True).then_inc(y_done, 1)

            def gram(i, lag, s):
                n, u = (parity(i) + lag) % 2, s // 2
                pe.wait_ge(norm_done, count(i, lag, BLOCKS, s + 1))
                if s == 0:
                    pe.wait_ge(x_done, count(i, lag, 1, 1))
                if s % 2 == 0:
                    await_(pe, gram_out, count(i, lag, 4, u - 1))
                for b in range(s * BS, (s + 1) * BS):
                    g, j = divmod(b, 4)
                    c = (g - 2 * u * BS // 4) * TC
                    mm = pe.matmul(gram_bank[u % 2][32 * j:32 * j + 32, c:c + TC], tt[n][:, b, 0:PR],
                                   tt[n][:, b, :], start=True, stop=True)
                if s == BLOCKS - 1:
                    for j in range(4):
                        mm = pe.matmul(gram_bank[1][32 * j:32 * j + 32, 384:384 + GR], ones[:],
                                       tt[n][:, j::4, PR], start=True, stop=True)
                mm.then_inc(gram_done, 1)

            def interact(i, ks):
                if ks[0] == 0:
                    pe.wait_ge(regrouped, count(i, 2, 256, 256))
                    await_(pe, yv_out, count(i, 2, 1, 0))
                for k in ks:
                    mm = pe.matmul(tower_bank[:], pairs[:, :, :, k].rearrange("p j g -> p (j g)"),
                                   wl_sb[:, k, :], start=(k == 0), stop=(k == QK))
                if ks[-1] == QK:
                    mm.then_inc(z_done, 1)

            def turn_z(i):
                pe.wait_ge(z_scaled, count(i, 3, 1, 1))
                for k in range(KO):
                    mm = pe.transpose(tower_bank[:, k * P:(k + 1) * P], z_n[:, k * P:(k + 1) * P], identity[:])
                mm.then_inc(zt_done, 1)

            def hidden1(i, ms):
                first = (i - 3) * P if isinstance(i, int) else pe.snap(i[0] * (2 * P) + (i[1] - 3) * P)
                if ms[0] == 0:
                    pe.wait_ge(zt_out, count(i, 3, 1, 1))
                for m in ms:
                    for k in range(KO + KD):
                        if k < KO:
                            rhs = z_t[:, k, :]
                        else:
                            rhs = dense_all[:, k - KO, bass.ds(first, P)].rearrange("p (g j) -> p j g", j=4)
                        mm = pe.matmul(tower_bank[:, m * P:(m + 1) * P], w1_sb[:, k, m * P:(m + 1) * P], rhs,
                                       start=(k == 0), stop=(k == KO + KD - 1))
                if ms[-1] == KH1 - 1:
                    mm.then_inc(h1_done, 1)

            def hidden2(i):
                pe.wait_ge(h1_out, count(i, 3, 1, 1))
                for m in range(KH2):
                    for k in range(KH1):
                        mm = pe.matmul(tower_bank[:, m * P:(m + 1) * P], w2_sb[:, k, m * P:(m + 1) * P],
                                       h1_t[:, k, :], start=(k == 0), stop=(k == KH1 - 1))
                mm.then_inc(h2_done, 1)

            def last_layer(i):
                pe.wait_ge(h2_out, count(i, 3, 1, 1))
                for k in range(KH2):
                    mm = pe.matmul(tower_bank[0:1, H2:H2 + P], w3_sb[:, k:k + 1], h2_t[:, k, :],
                                   start=(k == 0), stop=(k == KH2 - 1))
                mm.then_inc(yv_done, 1)

            def step(i, a, c, z, t):
                if c:
                    fold(i, 0)
                if z:
                    gram(i, 2, BLOCKS - 2)
                if a:
                    turn(i, (0, 1))
                if z:
                    gram(i, 2, BLOCKS - 1)
                if t:
                    turn_z(i)
                if a:
                    turn(i, (2, 3))
                if i == 2:
                    pe.wait_ge(s_wl_ready, 1)
                if i == 3:
                    pe.wait_ge(s_w1_ready, 1)
                    pe.wait_ge(s_dense, 16)
                for s in range(BLOCKS):
                    if c:
                        project(i, s)
                    if c and s in (0, 2, 4):
                        fold(i, s // 2 + 1)
                    if c and s >= 2:
                        gram(i, 1, s - 2)
                    if a and 1 <= s <= NG:
                        g_product(i, s - 1)
                    if t and s in (0, 1):
                        hidden1(i, (2 * s, 2 * s + 1))
                    if t and s == 2:
                        hidden2(i)
                    if t and s == 3:
                        last_layer(i)
                    if z and s in (4, 5, 6):
                        interact(i, {4: (0,), 5: (1, 2), 6: (3, 4)}[s])

            run_steps(pe, step)

        @block.scalar
        def _(act):
            act.wait_ge(s_wse_ps, 1)
            act.activation(ws_e[:], bank[0][:, 0:P], ACT.Copy).then_inc(s_wse, 1)
            act.wait_ge(s_gram_ps, 1)
            act.wait_ge(s_const, 1)
            for h in range(2):
                s = slice(h * D, (h + 1) * D)
                act.activation(gram_w[s, s], bank[1][s, s], ACT.Copy, scale=1.0 / E).then_inc(s_gramw, 1)

            def sqrt(dst, src, scale, done):
                act.activation(dst, src, ACT.Sqrt, bias=eps[:], scale=scale).then_inc(done, 1)

            def turn_out(i, groups):
                if groups[0] == 0:
                    await_(act, g_done, count(i, 0, NG, 0))
                for g in groups:
                    act.wait_ge(turned, count(i, 0, NG, g + 1))
                    k, n = GROUPS[g][0], len(GROUPS[g])
                    act.activation(emb_t[:, k:k + n, :].rearrange("p k r -> p (k r)"),
                                   feat_bank[g % 2][:, 0:n * P], ACT.Copy).then_inc(turned_out, 1)

            def x_root(i):
                act.activation(junk_x[:], feat_bank[1][:, P:2 * P], ACT.Square, accum_out=var_x[:]).then_inc(x_sq, 1)
                act.wait_ge(x_sq, count(i, 0, 1, 1))
                sqrt(std_x[:], var_x[:], 1.0 / E, x_std)

            def gram_copy(i, lag, u):
                act.wait_ge(gram_done, count(i, lag, BLOCKS, 2 * u + 2))
                if u == 0:
                    await_(act, regrouped, count(i, lag, 256, 0))
                g = GR // 4
                if u == 3:
                    act.activation(gram_s[:, 2, :, QK], gram_bank[1][:, 384:384 + GR], ACT.Copy)
                src = gram_bank[u % 2][:, 0:g * TC].rearrange("p (g q) -> p g q", q=TC)
                dst = gram_s[:, :, u * g:(u + 1) * g, :]
                act.activation(dst[:, :, :, 0:QK].rearrange("p r g k -> p g k r"),
                               src[:, :, 0:SL].rearrange("p g (k r) -> p g k r", r=4), ACT.Copy)
                act.activation(dst[:, 0:2, :, QK].rearrange("p r g -> p g r"), src[:, :, PR:TC],
                               ACT.Copy).then_inc(gram_low, 1)

            def fold_up(i, m):
                act.wait_ge(fold_done, count(i, 1, NF, m + 1))
                for h in range(2):
                    act.activation(folded[0:D, h, m, :], fold_bank[h * D:(h + 1) * D, :],
                                   ACT.Copy).then_inc(fold_high, 1)

            def step(i, a, c, z, t):
                if c:
                    await_(act, y_done, count(i, 1, BLOCKS, 0))
                    fold_up(i, 0)
                if a:
                    turn_out(i, (0, 1))
                if z:
                    gram_copy(i, 2, 3)
                if t:
                    act.wait_ge(zt_done, count(i, 3, 1, 1))
                    act.activation(z_t[:].rearrange("p k b -> p (k b)"), tower_bank[:, 0:OU],
                                   ACT.Copy).then_inc(zt_out, 1)
                if a:
                    turn_out(i, (2, 3))
                    x_root(i)
                for s in range(BLOCKS):
                    if c:
                        act.wait_ge(y_done, count(i, 1, BLOCKS, s + 1))
                        await_(act, var_done, count(i, 1, BLOCKS, s - 1))
                        act.activation(square[s % 2][:].rearrange("p s q -> p (s q)"), y_bank[s % 2][:],
                                       ACT.Square).then_inc(sq_done, 1)
                    if c and s in (0, 2, 4):
                        fold_up(i, s // 2 + 1)
                    if a and s == 1:
                        act.wait_ge(x_rstd, count(i, 0, 1, 1))
                        act.activation(x_n[:], feat_bank[1][:, P:2 * P], ACT.Copy,
                                       scale=rstd_x[:]).then_inc(x_scaled, 1)
                    if t and s == 2:
                        act.wait_ge(h1_done, count(i, 3, 1, 1))
                        for m in range(KH1):
                            ins = act.activation(h1_t[:, m, :], tower_bank[:, m * P:(m + 1) * P], ACT.Relu,
                                                 bias=b1_sb[:, m:m + 1])
                        ins.then_inc(h1_out, 1)
                    if t and s == 3:
                        act.wait_ge(h2_done, count(i, 3, 1, 1))
                        for m in range(KH2):
                            ins = act.activation(h2_t[:, m, :], tower_bank[:, m * P:(m + 1) * P], ACT.Relu,
                                                 bias=b2_sb[:, m:m + 1])
                        ins.then_inc(h2_out, 1)
                    if a and s == 6:
                        act.wait_ge(var1_done, count(i, 0, 1, 1))
                        sqrt(std1[:], var1[:], 1.0, std1_done)
                    if c:
                        act.wait_ge(var_done, count(i, 1, BLOCKS, s + 1))
                        sqrt(std2[s % 2][:], var2[s % 2][:], 1.0 / PR, std_done)
                    if t and s == 4:
                        first = (i - 3) * P if isinstance(i, int) else act.snap(i[0] * (2 * P) + (i[1] - 3) * P)
                        act.wait_ge(yv_done, count(i, 3, 1, 1))
                        act.activation(y_all[0:1, bass.ds(first, P)].rearrange("o (g j) -> o j g", j=4),
                                       tower_bank[0:1, H2:H2 + P].rearrange("o (j g) -> o j g", j=4),
                                       ACT.Copy).then_inc(yv_out, 1)
                    if c and s in (4, 6):
                        gram_copy(i, 1, (4, 6).index(s))
                    if z and s == 7:
                        act.wait_ge(z_done, count(i, 2, 1, 1))
                        act.activation(junk_z[:], tower_bank[:], ACT.Square, accum_out=var3[:]).then_inc(z_sq, 1)
                        act.wait_ge(z_sq, count(i, 2, 1, 1))
                        sqrt(std3[:], var3[:], 1.0 / O, z_std)
                if c:
                    gram_copy(i, 1, 2)
                if z:
                    act.wait_ge(z_rstd, count(i, 2, 1, 1))
                    act.activation(z_n[:], tower_bank[:, 0:OU], ACT.Copy, scale=rstd3[:]).then_inc(z_scaled, 1)

            run_steps(act, step)

        @block.vector
        def _(dve):
            done = [0]

            def link(ins):
                done[0] += 1
                ins.then_inc(s_prep, 1)
                dve.wait_ge(s_prep, done[0])

            def centre(w, mean, width):
                link(dve.tensor_reduce(mean, w, AX.X, ALU.add))
                link(dve.tensor_scalar(mean, mean, 1.0 / width, None, ALU.mult))
                link(dve.tensor_tensor(w, w, mean.unsqueeze(2).broadcast_to(list(w.shape)), ALU.subtract))

            dve.wait_ge(s_ids, 32)
            dve.tensor_tensor(ids_all[:].rearrange("p (t c) -> p t c", c=2 * CH),
                              ids_all[:].rearrange("p (t c) -> p t c", c=2 * CH),
                              off_sb[:].unsqueeze(1).broadcast_to([P, TILES, 2 * CH]),
                              ALU.add).then_inc(s_ids_ready, 1)
            dve.memset(eps[:], EPS)
            dve.memset(ones[:], 1.0)
            dve.memset(tt[0][:, :, PR + 1:TC], 1.0)
            dve.memset(tt[1][:, :, PR + 1:TC], 1.0)
            dve.memset(gram_s[:, 3, :, QK], 1.0)
            link(dve.memset(mix_w[:], 0.0))
            dve.memset(gram_w[:], 0.0).then_inc(s_const, 1)
            dve.wait_ge(s_ws, 16 * len(WS))
            centre(ws_sb[:].unsqueeze(1), mean_a[:], E)
            dve.tensor_tensor(wg_sb[:], ws_sb[:], gs_sb[:], ALU.mult).then_inc(s_ws_ready, 1)
            dve.wait_ge(s_wsi, 16 * len(WSI))
            centre(wsi_sb[:], mean_b[:], PR)
            dve.tensor_scalar(mean_a[:], mean_a[:], 1.0, None, ALU.mult).then_inc(s_wsi_ready, 1)
            dve.tensor_tensor(fold_w[:], wsi_sb[:].unsqueeze(2).broadcast_to([P, CH, SPAN, PR]),
                              owner_sb[:].unsqueeze(3).broadcast_to([P, CH, SPAN, PR]),
                              ALU.mult).then_inc(s_fold_ready, 1)
            centre(wd_sb[:], mean_c[:], E)
            dve.tensor_scalar(mean_a[:], mean_a[:], 1.0, None, ALU.mult).then_inc(s_wd_ready, 1)
            dve.wait_ge(s_wsum_ps, 1)
            link(dve.tensor_copy(wsum_row[:], bank[2][0:1, 0:PR].unsqueeze(1).broadcast_to([1, BS, PR])))
            wsum = wsum_row[:].rearrange("o s q -> o (s q)")
            dve.tensor_copy(bs_parts[:, 0, :], bs_row[:])
            dve.tensor_copy(wg_hi[:], wg_sb[:])
            link(dve.tensor_copy(wsum_parts[:, 0, :], wsum))
            dve.tensor_tensor(bs_parts[:, 1, :], bs_row[:], bs_parts[:, 0, :], ALU.subtract)
            dve.tensor_tensor(wg_lo[:], wg_sb[0:D, :], wg_hi[0:D, :], ALU.subtract)
            dve.tensor_tensor(wsum_parts[:, 1, :], wsum, wsum_parts[:, 0, :], ALU.subtract).then_inc(s_parts, 1)
            dve.wait_ge(s_small, 16 * len(SMALL))
            for dst, u, v in ((gg, gp, gq), (gb, gp, bq), (bg, bp, gq), (bb, bp, bq)):
                link(dve.tensor_scalar(dst[:], v[:], u[:], None, ALU.mult))
            link(dve.tensor_scalar(mix_w[:, 0:QK, 96], bb[:], float(E), None, ALU.mult))
            link(dve.tensor_copy(mix_w[:, QK, 64:65], bp[:]))
            for k in range(QK):
                link(dve.tensor_scalar(mix_w[:, k, PR:2 * PR], eye_p_sb[:], gb[:, k:k + 1], None, ALU.mult))
                link(dve.scalar_tensor_tensor(out=mix_w[:, k, PR:2 * PR], in0=eye_q_sb[:, k, :],
                                              scalar=bg[:, k:k + 1], in1=mix_w[:, k, PR:2 * PR],
                                              op0=ALU.mult, op1=ALU.add))
            dve.wait_ge(s_wl, 16)
            centre(wl_sb[:], mean_d[:], O)
            dve.tensor_scalar(mean_a[:], mean_a[:], 1.0, None, ALU.mult).then_inc(s_mix_ready, 1)
            dve.wait_ge(s_mix_ps, 1)
            for k in range(QK):
                dve.tensor_scalar(wl_sb[:, k, :], wl_sb[:, k, :], gg[:, k:k + 1], None, ALU.mult)
            dve.tensor_scalar(wl_sb[0:PR, QK, :], wl_sb[0:PR, QK, :], gp[0:PR, :], None, ALU.mult)
            for r in (1, 2):
                dve.tensor_copy(wl_sb[r * PR:(r + 1) * PR, QK, :], bank[4][r * PR:(r + 1) * PR, :])
            dve.tensor_copy(wl_sb[3 * PR:P, QK, :], bank[4][3 * PR:P, :]).then_inc(s_wl_ready, 1)
            dve.wait_ge(s_b1_ps, 1)
            for k in range(KO):
                dve.tensor_scalar(w1_sb[:, k, :], w1_sb[:, k, :], gl_sb[:, k:k + 1], None, ALU.mult)
            dve.tensor_tensor(b1_sb[:], b1_sb[:], bank[3][:, 0:KH1], ALU.add).then_inc(s_w1_ready, 1)

            def products(i, g):
                chunks = GROUPS[g]
                dve.wait_ge(g_done, count(i, 0, NG, g + 1))
                sl = slice(chunks[0], chunks[-1] + 1)
                dve.tensor_tensor(prod[:, sl, :, :].rearrange("p k h d -> p (k h d)"),
                                  feat_bank[g % 2][:, 0:len(chunks) * P],
                                  emb[parity(i)][:, sl, :, :].rearrange("p k h d -> p (k h d)"),
                                  ALU.mult).then_inc(prod_done, 1)

            def gram_pick(i, lag, u):
                dve.wait_ge(gram_low, count(i, lag, 4, u + 1))
                dve.tensor_copy(wait_carrier_v[:, u:u + 1], eps[:])
                g = GR // 4
                src = gram_bank[u % 2][:, 0:g * TC].rearrange("p (g q) -> p g q", q=TC)
                dve.copy_predicated(
                    gram_s[:, :, u * g:(u + 1) * g, 0:QK].rearrange("p r g k -> p g k r"),
                    take_upper[:].rearrange("p (k r) -> p k r", r=4).unsqueeze(1).broadcast_to([P, g, QK, 4]),
                    src[:, :, SL:PR].rearrange("p g (k r) -> p g k r", r=4)).then_inc(gram_out, 1)

            def fold_rest(i, m):
                dve.wait_ge(fold_high, count(i, 1, 2 * NF, 2 * m + 2))
                for h in range(2):
                    low = dve.tensor_tensor(folded[D:P, h, m, :], fold_bank[h * D:(h + 1) * D, :],
                                            folded[0:D, h, m, :], ALU.subtract)
                low.then_inc(fold_out, 1)

            def step(i, a, c, z, t):
                if c:
                    fold_rest(i, 0)
                if z:
                    gram_pick(i, 2, 3)
                if a:
                    dve.wait_ge(x_std, count(i, 0, 1, 1))
                    dve.reciprocal(rstd_x[:], std_x[:]).then_inc(x_rstd, 1)
                for s in range(BLOCKS):
                    if c:
                        dve.wait_ge(sq_done, count(i, 1, BLOCKS, s + 1))
                        dve.tensor_reduce(var2[s % 2][:], square[s % 2][:], AX.X, ALU.add).then_inc(var_done, 1)
                    if c and s in (0, 2, 4):
                        fold_rest(i, s // 2 + 1)
                    if a and s == 5:
                        dve.wait_ge(prod_done, count(i, 0, NG, NG))
                        dve.tensor_reduce(var1[:], prod[:], AX.X, ALU.add).then_inc(var1_done, 1)
                    if c:
                        dve.wait_ge(std_done, count(i, 1, BLOCKS, s + 1))
                        dve.reciprocal(rstd2[s % 2][:], std2[s % 2][:]).then_inc(rstd_done, 1)
                        dve.wait_ge(rstd_done, count(i, 1, BLOCKS, s + 1))
                        dve.tensor_tensor(tt[parity(i) ^ 1][:, s * BS:(s + 1) * BS, 0:PR],
                                          y_bank[s % 2][:].rearrange("p (s q) -> p s q", q=PR),
                                          rstd2[s % 2][:].unsqueeze(2).broadcast_to([P, BS, PR]),
                                          ALU.mult).then_inc(norm_done, 1)
                    if a and 1 <= s <= NG:
                        products(i, s - 1)
                    if a and s == NG:
                        await_(dve, gram_done, count(i, 1, BLOCKS, 0))
                        dve.tensor_scalar(tt[parity(i)][:, :, PR], feat_bank[1][:, P:2 * P], gd_sb[:], bd_sb[:],
                                          ALU.mult, ALU.add).then_inc(x_done, 1)
                    if c and s in (4, 6):
                        gram_pick(i, 1, (4, 6).index(s))
                    if a and s == 6:
                        dve.wait_ge(std1_done, count(i, 0, 1, 1))
                        dve.reciprocal(rstd1[:], std1[:]).then_inc(rstd1_done, 1)
                        dve.wait_ge(rstd1_done, count(i, 0, 1, 1))
                        await_(dve, fold_done, count(i, 0, NF, 0))
                        dve.tensor_tensor(emb_n[:], emb[parity(i)][:],
                                          rstd1[:].unsqueeze(3).broadcast_to([P, CH, 2, D]),
                                          ALU.mult).then_inc(emb_scaled, 1)
                if z:
                    dve.wait_ge(z_std, count(i, 2, 1, 1))
                    dve.reciprocal(rstd3[:], std3[:]).then_inc(z_rstd, 1)
                if c:
                    gram_pick(i, 1, 2)

            run_steps(dve, step)


def kernel(**inputs):
    from concourse import bacc
    from concourse.bass_utils import run_bass_kernel_spmd

    a = {k: np.asarray(v) for k, v in inputs.items()}
    row = np.arange(CH * P).reshape(CH, P)
    feat = (row % NS).T
    owner = (row // NS).T - (np.arange(CH) * P // NS)[None, :]
    base = np.concatenate([[0], np.cumsum(VOCAB)[:-1]])
    by_half = a["ids"].astype(np.int32, copy=False).reshape(TILES, NF, 2, BS * NS).transpose(0, 2, 1, 3)
    by_chunk = by_half.reshape(TILES, 2, CH, P).transpose(3, 0, 2, 1)
    offsets = np.repeat(base[feat][:, :, None], 2, axis=2).reshape(P, 2 * CH)

    pr = np.arange(P)[:, None] % PR
    slot = 4 * np.arange(QK)[None, :] + (np.arange(P) // PR)[:, None]
    far = (pr % SL < slot) == (pr >= SL)
    q = slot + SL * far
    wl_t = a["L0_rec_Wl"].T
    wl = np.zeros((P, QK + 1, O), wl_t.dtype)
    hi, lo = np.maximum(pr, q) + 1, np.minimum(pr, q) + 1
    rr, kk = np.nonzero((pr % SL != slot) | (pr < SL))
    wl[rr, kk] = wl_t[(hi * (hi - 1) // 2 + lo)[rr, kk]]
    row_p, all_slots = np.arange(P)[:, None] % PR, np.arange(SL)[None, :]
    upper = (row_p % SL < all_slots) == (row_p >= SL)
    pr = pr[:, 0]
    first = np.arange(1, PR + 1)
    wl[0:PR, QK] = wl_t[first * (first - 1) // 2]

    def cols(v, n):
        return v.reshape(n, P).T

    f = np.float32
    args = {
        "table": np.concatenate([a[f"tbl_{n}"] for n in range(NS)]),
        "ids": by_chunk.reshape(P, TILES * 2 * CH),
        "offsets": offsets.astype(np.int32),
        "dense_t": a["r_dense_t"].T,
        "ident": np.eye(P, dtype=f),
        "ws_t": np.concatenate([a["L0_rec_Ws"].T] * 2),
        "gs": np.broadcast_to(a["L0_rec_gs"], (P, E)),
        "bs": a["L0_rec_bs"][None],
        "wsi": a["L0_rec_Wsi"].T[feat],
        "owner": (owner[:, :, None] == np.arange(SPAN)).astype(f),
        "wd_t": a["L0_rec_Wd"].T.reshape(KD, P, E).transpose(1, 0, 2),
        "gd": a["L0_rec_gd"][:, None], "bd": a["L0_rec_bd"][:, None],
        "wl": wl,
        "gsi_p": a["L0_rec_gsi"][pr][:, None], "gsi_q": a["L0_rec_gsi"][q],
        "bsi_p": a["L0_rec_bsi"][pr][:, None], "bsi_q": a["L0_rec_bsi"][q],
        "eye_p": (pr[:, None] == np.arange(PR)).astype(f),
        "eye_q": (q[:, :, None] == np.arange(PR)).astype(f),
        "w1": np.concatenate([a["W_top1"][:OU], a["W_top1"][O:]]).reshape(KO + KD, P, H1).transpose(1, 0, 2),
        "gl": cols(a["L0_rec_gl"][:OU], KO), "bl": cols(a["L0_rec_bl"][:OU], KO),
        "b1": cols(a["b_top1"], KH1),
        "w2": a["W_top2"].reshape(KH1, P, H2).transpose(1, 0, 2),
        "b2": cols(a["b_top2"], KH2),
        "upper": upper.astype(np.int32),
        "w3": a["W_top3"].reshape(KH2, P).T,
    }
    nc = bacc.Bacc("TRN2", target_bir_lowering=False, num_devices=1)
    args = {k: np.ascontiguousarray(v) for k, v in args.items()}
    aps = {k: nc.dram_tensor(f"in_{k}", v.shape, mybir.dt.from_np(v.dtype), kind="ExternalInput").ap()
           for k, v in args.items()}
    out = nc.dram_tensor("out_y", (B, 1), F32, kind="ExternalOutput").ap()
    build_tower(nc, **aps, out=out)
    r = run_bass_kernel_spmd(nc, [{f"in_{k}": v for k, v in args.items()}], core_ids=[0])
    return r.results[0]["out_y"]
```

```python
from contextlib import ExitStack

import numpy as np

import concourse.bass as bass
from concourse import mybir

ALU = mybir.AluOpType
ACT = mybir.ActivationFunctionType
AX = mybir.AxisListType
F32 = mybir.dt.float32
I32 = mybir.dt.int32
F16 = mybir.dt.float16

P = 128
VOCAB = [12500, 125000, 12500, 1250, 12500, 125000, 125000, 1000, 12500, 12500, 1250, 1250, 1250,
         1250, 12500, 12500, 12500, 1250, 1250, 1000, 1000, 1000, 1000, 1000, 1000, 1000]
B = 2048
NS = len(VOCAB)
D = 64
DD = 256
E = 128
PR = 32
O = 512
OU = 384
H1, H2 = 512, 256
EPS = 1e-5
UP = 64

TILES = B // P
HALF = P // 2
CH = HALF * NS // P
SPAN = 6
BS = 16
BLOCKS = P // BS
GR = P // 4
SL = PR // 2
QK = SL // 4
TC = PR + 2
KD, KO, KH1, KH2 = DD // P, OU // P, H1 // P, H2 // P

GROUPS = [range(0, 4), range(4, 8), range(8, 12), range(12, 13)]
NG = len(GROUPS)
PARTS = [slice(0, 8), slice(8, CH)]


def samples_of(k):
    return k * P // NS, (k * P + P - 1) // NS


def fold_plan(m):
    plan = []
    for k in range(CH):
        a, b = samples_of(k)
        a, b = max(a, m * BS), min(b, m * BS + BS - 1)
        if a <= b:
            plan.append((k, a, b - a + 1))
    return plan


FOLDS = [fold_plan(m) for m in range(HALF // BS)]
NF = len(FOLDS)

G_SLOT = [1, 2, 3, 4]
FOLD_SLOT = [1, 2, 4]
VAR_SLOT = (3, 0)
SCALE_SLOT = (5, 1)


def count(step, lag, per_tile, k):
    if isinstance(step, int):
        return (step - lag) * per_tile + k
    pair, odd = step
    return pair * (2 * per_tile) + ((odd - lag) * per_tile + k)


def await_(eng, sem, value):
    if isinstance(value, int) and value <= 0:
        return
    eng.wait_ge(sem, value)


def parity(step):
    return step % 2 if isinstance(step, int) else step[1]


def run_steps(eng, step_fn):
    for i in range(4):
        step_fn(i, True, i >= 1, i >= 2, i >= 3)
    with eng.Fori(2, TILES // 2) as pair:
        step_fn((pair, 0), True, True, True, True)
        step_fn((pair, 1), True, True, True, True)
    step_fn(TILES, False, True, True, True)
    step_fn(TILES + 1, False, False, True, True)
    step_fn(TILES + 2, False, False, False, True)


def build_tower(nc, table, ids, offsets, dense_t, ident, ws_t, gs, bs, wsi, owner, wd_t, gd, bd,
                wl, gsi_p, gsi_q, bsi_p, bsi_q, eye_p, eye_q, w1, gl, bl, b1, w2, b2, w3, upper, out):
    with ExitStack() as ctx:
        def sb(name, shape, dt=F32):
            return ctx.enter_context(nc.sbuf_tensor(name, shape, dt))

        def sem(name):
            return ctx.enter_context(nc.semaphore(name))

        bank = [ctx.enter_context(nc.psum_tensor(f"bank{n}", [P, 512], F32)) for n in range(8)]
        feat_bank = bank[0:2]
        fold_bank = bank[2]
        tower_bank = bank[3]
        y_bank = bank[4:6]
        gram_bank = bank[6:8]

        identity = sb("identity", [P, P])
        eps, eps_z = sb("eps", [P, 1]), sb("eps_z", [P, 1])
        ones = sb("ones", [P, PR])
        ids_all = sb("ids_all", [P, TILES * 2 * CH], I32)
        off_sb = sb("off_sb", [P, 2 * CH], I32)
        ws_sb = sb("ws_sb", [P, E])
        gs_sb = sb("gs_sb", [P, E])
        wg_sb = sb("wg_sb", [P, E])
        ws_e = sb("ws_e", [P, P])
        gram_w = sb("gram_w", [P, P])
        wg_hi = sb("wg_hi", [P, E], F16)
        wg_lo = sb("wg_lo", [D + 3, E], F16)
        bs_row = sb("bs_row", [1, E])
        wsum_row = sb("wsum_row", [1, BS, PR])
        bs_parts = sb("bs_parts", [1, 2, E], F16)
        wsum_parts = sb("wsum_parts", [1, 2, BS * PR], F16)
        wsi_sb = sb("wsi_sb", [P, CH, PR])
        owner_sb = sb("owner_sb", [P, CH, SPAN])
        fold_w = sb("fold_w", [P, CH, SPAN, PR])
        wd_sb = sb("wd_sb", [P, KD, E])
        gd_sb, bd_sb = sb("gd_sb", [P, 1]), sb("bd_sb", [P, 1])
        wl_sb = sb("wl_sb", [P, QK + 1, O])
        gp, gq = sb("gp", [P, 1]), sb("gq", [P, QK])
        bp, bq = sb("bp", [P, 1]), sb("bq", [P, QK])
        gg, gb, bg, bb = (sb(n, [P, QK]) for n in ("gg", "gb", "bg", "bb"))
        eye_p_sb = sb("eye_p_sb", [P, PR])
        eye_q_sb = sb("eye_q_sb", [P, QK, PR])
        take_upper = sb("take_upper", [P, SL], I32)
        mix_w = sb("mix_w", [P, QK + 1, P])
        wl_hi, wl_lo = sb("wl_hi", [P, QK + 1, O], F16), sb("wl_lo", [P, QK + 1, O], F16)
        w1_sb = sb("w1_sb", [P, KO + KD, H1])
        w1_hi, w1_lo = sb("w1_hi", [P, KO + KD, H1], F16), sb("w1_lo", [P, KO + KD, H1], F16)
        gl_sb, bl_sb = sb("gl_sb", [P, KO]), sb("bl_sb", [P, KO])
        b1_sb, b2_sb = sb("b1_sb", [P, KH1]), sb("b2_sb", [P, KH2])
        w2_sb = sb("w2_sb", [P, KH1, H2])
        w3_sb = sb("w3_sb", [P, KH2])
        mean_a, mean_b = sb("mean_a", [P, 1]), sb("mean_b", [P, CH])
        mean_c, mean_d = sb("mean_c", [P, KD]), sb("mean_d", [P, QK + 1])
        dense_hi, dense_lo = sb("dense_hi", [P, KD, B], F16), sb("dense_lo", [P, KD, B], F16)

        wait_carrier_v = sb("wait_carrier_v", [P, 4])
        wait_carrier = sb("wait_carrier", [P, 2], I32)
        rows_id = [sb(f"rows_id{n}", [P, 2 * CH], I32) for n in range(2)]
        emb = [sb(f"emb{n}", [P, CH, 2, D]) for n in range(2)]
        dense_in = [sb(f"dense_in{n}", [P, KD, P]) for n in range(2)]
        emb_t = sb("emb_t", [P, CH, P])
        prod = sb("prod", [P, CH, 2, D])
        var1, std1, rstd1 = (sb(n, [P, CH, 2]) for n in ("var1", "std1", "rstd1"))
        emb_n = sb("emb_n", [P, CH, 2, D])
        junk_x = sb("junk_x", [P, E])
        var_x, std_x, rstd_x = (sb(n, [P, 1]) for n in ("var_x", "std_x", "rstd_x"))
        x_n = sb("x_n", [P, E])
        folded = sb("folded", [P, 2, NF, BS * PR], F16)
        folded_b = sb("folded_b", [D + 3, 2, NF, BS * PR], F16)
        square = [sb(f"square{n}", [P, BS, PR]) for n in range(2)]
        var2 = [sb(f"var2_{n}", [P, BS]) for n in range(2)]
        std2 = [sb(f"std2_{n}", [P, BS]) for n in range(2)]
        rstd2 = [sb(f"rstd2_{n}", [P, BS]) for n in range(2)]
        tt = [sb(f"tt{n}", [P, P, TC]) for n in range(2)]
        dense_all = tt[1][:].rearrange("p b q -> p (b q)")[:, 0:KD * B].rearrange("p (k b) -> p k b", b=B)
        gram_s = sb("gram_s", [P, 4, GR, QK + 1])
        pairs = sb("pairs", [P, 4, GR, QK + 1])
        pairs_hi = sb("pairs_hi", [P, 4, GR, QK + 1], F16)
        pairs_lo = sb("pairs_lo", [P, 4, GR, QK + 1], F16)
        junk_z = sb("junk_z", [P, O])
        var3, std3, rstd3 = (sb(n, [P, 1]) for n in ("var3", "std3", "rstd3"))
        z_n = sb("z_n", [P, OU])
        z_hi, z_lo = sb("z_hi", [P, KO, P], F16), sb("z_lo", [P, KO, P], F16)
        h1_t = sb("h1_t", [P, KH1, P])
        h2_t = sb("h2_t", [P, KH2, P])
        y_all = sb("y_all", [1, B])

        s_ids, s_small, s_ws, s_wsi, s_wl, s_w1, s_dense = (
            sem(n) for n in ("ids_in", "small_in", "ws_in", "wsi_in", "wl_in", "w1_in", "dense_in_all"))
        dense_got = [sem(f"dense_got{n}") for n in range(2)]
        s_ids_ready, s_prep, s_ws_ready, s_wse_ps, s_wse, s_gram_ps, s_gramw = (
            sem(n) for n in ("ids_ready", "prep_step", "ws_ready", "wse_ps", "wse", "gramw_ps", "gramw"))
        s_wsi_ready, s_wsum_ps, s_fold_ready, s_wd_ready = (
            sem(n) for n in ("wsi_ready", "wsum_ps", "fold_ready", "wd_ready"))
        s_mix_ready, s_mix_ps, s_wl_ready, s_b1_ps, s_w1_ready, s_const, s_parts, s_bias = (
            sem(n) for n in ("mix_ready", "mix_ps", "wl_ready", "b1_ps", "w1_ready", "const_ready",
                             "parts_ready", "bias_rows_in"))
        highs, parts = sem("highs_made"), sem("parts_made")
        slot_ids = sem("slot_ids")
        gathered = [sem(f"gathered{n}") for n in range(2)]
        turned, turned_out = sem("turned"), sem("turned_out")
        x_sq, x_std, x_rstd, x_scaled, x_done = (
            sem(n) for n in ("x_sq", "x_std", "x_rstd", "x_scaled", "x_done"))
        g_done, prod_done = sem("g_done"), sem("prod_done")
        var1_done, std1_done, rstd1_done, emb_scaled = (
            sem(n) for n in ("var1_done", "std1_done", "rstd1_done", "emb_scaled"))
        fold_done, fold_out = sem("fold_done"), sem("fold_out")
        fold_high, fold_again = sem("fold_high"), sem("fold_again")
        y_done, sq_done, var_done, std_done, rstd_done, norm_done, gram_done = (
            sem(n) for n in ("y_done", "sq_done", "var_done", "std_done", "rstd_done", "norm_done",
                             "gram_done"))
        pairs_high, pairs_out = sem("pairs_high"), sem("pairs_out")
        gram_low, gram_out = sem("gram_low"), sem("gram_out")
        regrouped = sem("regrouped")
        z_done, z_sq, z_std, z_rstd, z_scaled, zt_done, zt_out = (
            sem(n) for n in ("z_done", "z_sq", "z_std", "z_rstd", "z_scaled", "zt_done", "zt_out"))
        z_parts = sem("z_parts")
        h1_done, h1_out, h2_done, h2_out, yv_done, yv_out = (
            sem(n) for n in ("h1_done", "h1_out", "h2_done", "h2_out", "yv_done", "yv_out"))
        stored = sem("stored")

        SMALL = [(identity, ident), (gd_sb, gd), (bd_sb, bd), (gp, gsi_p), (gq, gsi_q), (bp, bsi_p),
                 (bq, bsi_q), (eye_p_sb, eye_p), (eye_q_sb, eye_q), (gl_sb, gl), (bl_sb, bl),
                 (b1_sb, b1), (b2_sb, b2), (w3_sb, w3), (take_upper, upper)]
        WS = [(ws_sb, ws_t), (gs_sb, gs), (bs_row, bs)]
        WSI = [(wsi_sb, wsi), (owner_sb, owner), (wd_sb, wd_t)]
        dense_tiles = dense_t.rearrange("(c k) b -> k c b", k=P)

        block = ctx.enter_context(nc.Block())

        def by_residue(parts_of, k):
            return parts_of[:, k, :].rearrange("p (t j g) -> p t j g", j=4, g=GR)

        def from_sample(k):
            return dense_all[:, k, :].rearrange("p (t g j) -> p t j g", j=4, g=GR)

        @block.sync
        def _(sp):
            sp.dma_start(ids_all[:], ids[:, :]).then_inc(s_ids, 16)
            sp.dma_start(off_sb[:], offsets[:, :]).then_inc(s_ids, 16)
            for dst, src in WS:
                sp.dma_start(dst[:], src).then_inc(s_ws, 16)
            for dst, src in SMALL:
                sp.dma_start(dst[:], src).then_inc(s_small, 16)
            for dst, src in WSI:
                sp.dma_start(dst[:], src).then_inc(s_wsi, 16)
            sp.dma_start(dense_in[0][:], dense_tiles[:, :, 0:P]).then_inc(dense_got[0], 16)
            sp.dma_start(wl_sb[:], wl).then_inc(s_wl, 16)
            sp.dma_start(w1_sb[:], w1).then_inc(s_w1, 16)
            sp.dma_start(w2_sb[:], w2).then_inc(s_w1, 16)
            sp.dma_start(dense_all, dense_tiles).then_inc(s_dense, 16)

            sp.wait_ge(s_parts, 1)
            for row, (u, v) in enumerate([(0, 0), (0, 1), (1, 0)]):
                sp.dma_start(wg_lo[D + row:D + row + 1, :], bs_parts[:, u, :]).then_inc(s_bias, 16)
                for h in range(2):
                    sp.dma_start(folded_b[D + row:D + row + 1, h, :, :],
                                 wsum_parts[:, v, :].unsqueeze(1).broadcast_to([1, NF, BS * PR])).then_inc(s_bias, 16)

            def held(value):
                return value if isinstance(value, int) else sp.snap(value)

            def step(i, a, c, z, t):
                nxt = i + 1 if isinstance(i, int) else i[0] * 2 + (i[1] + 1)
                if not isinstance(i, int) or nxt < TILES:
                    first, free = held(nxt * P), held(count(i, 0, NG, 0))
                    await_(sp, turned, free)
                    dst = dense_in[1 - parity(i)]
                    sp.dma_start(dst[:], dense_tiles[:, :, bass.ds(first, P)]).then_inc(
                        dense_got[1 - parity(i)], 16)
                if z:
                    sp.wait_ge(gram_out, count(i, 2, 4, 4))
                    for j in range(4):
                        for r in range(4):
                            sp.dma_start(pairs[32 * r:32 * r + 32, j, :, :],
                                         gram_s[32 * j:32 * j + 32, r, :, :]).then_inc(regrouped, 16)

            for i in range(4):
                step(i, True, i >= 1, i >= 2, i >= 3)
            with sp.Fori(2, TILES // 2 - 1) as pair:
                step((pair, 0), True, True, True, True)
                step((pair, 1), True, True, True, True)
            step(TILES - 2, True, True, True, True)
            step(TILES - 1, True, True, True, True)
            step(TILES, False, True, True, True)
            step(TILES + 1, False, False, True, True)
            sp.wait_ge(yv_out, TILES)
            sp.dma_start(out.rearrange("n o -> o n"), y_all[:]).then_inc(stored, 16)
            sp.wait_ge(stored, 16)

        def gather_value(i, more):
            each = 16 * 2 * CH
            return (i // 2 + more) * each if isinstance(i, int) else i[0] * each + more * each

        @block.gpsimd
        def _(pool):
            def gather(i):
                n = parity(i)
                col = i * (2 * CH) if isinstance(i, int) else i[0] * (4 * CH) + i[1] * 2 * CH
                await_(pool, emb_scaled, count(i, 2, 2, 1))
                await_(pool, gathered[n], gather_value(i, 0))
                pool.tensor_copy(rows_id[n][:], ids_all[:, bass.ds(col, 2 * CH)]).then_inc(slot_ids, 1)
                pool.wait_ge(slot_ids, count(i, 0, 1, 1))
                pool.tensor_tensor(wait_carrier[:, 0:1], off_sb[:, 0:1], off_sb[:, 0:1], ALU.add)
                for k in range(CH):
                    if k == PARTS[1].start and (not isinstance(i, int) or i >= 2):
                        pool.wait_ge(emb_scaled, count(i, 2, 2, 2))
                        pool.tensor_tensor(wait_carrier[:, 1:2], off_sb[:, 0:1], off_sb[:, 0:1], ALU.add)
                    for h in range(2):
                        pool.indirect_dma_start(
                            emb[n][:, k, h, :], None, table[:, :],
                            bass.IndirectOffsetOnAxis(ap=rows_id[n][:, 2 * k + h:2 * k + h + 1], axis=0),
                        ).then_inc(gathered[n], 16)

            pool.wait_ge(s_ids_ready, 1)
            gather(0)
            gather(1)
            with pool.Fori(1, TILES // 2) as pair:
                gather((pair, 0))
                gather((pair, 1))

        @block.tensor
        def _(pe):
            pe.wait_ge(s_small, 16 * len(SMALL))
            pe.wait_ge(s_ws_ready, 1)
            pe.transpose(bank[0][:, 0:P], ws_sb[:], identity[:]).then_inc(s_wse_ps, 1)
            pe.wait_ge(s_wse, 1)
            pe.matmul(bank[1][:, 0:P], ws_e[:], ws_e[:], start=True, stop=True).then_inc(s_gram_ps, 1)
            pe.wait_ge(s_wsi_ready, 1)
            pe.matmul(bank[2][0:1, 0:PR], owner_sb[:, 0, 0:1], wsi_sb[:, 0, :], start=True,
                      stop=True).then_inc(s_wsum_ps, 1)
            pe.wait_ge(s_w1, 32)
            for m in range(KH1):
                for k in range(KO):
                    mm = pe.matmul(bank[3][:, m:m + 1], w1_sb[:, k, m * P:(m + 1) * P], bl_sb[:, k:k + 1],
                                   start=(k == 0), stop=(k == KO - 1))
            mm.then_inc(s_b1_ps, 1)
            pe.wait_ge(s_mix_ready, 1)
            for k in range(QK + 1):
                mm = pe.matmul(bank[4][:], mix_w[:, k, :], wl_sb[:, k, :], start=(k == 0),
                               stop=(k == QK))
            mm.then_inc(s_mix_ps, 1)
            pe.wait_ge(s_gramw, 2)
            pe.wait_ge(s_fold_ready, 1)
            pe.wait_ge(s_bias, 144)
            pe.wait_ge(s_wd_ready, 1)
            pe.wait_ge(s_const, 1)

            def turn(i, groups):
                n = parity(i)
                if groups[0] == 0:
                    pe.wait_ge(gathered[n], gather_value(i, 1))
                for g in groups:
                    chunks = GROUPS[g]
                    if g < 2:
                        await_(pe, prod_done, count(i, 0, NG, g - 1))
                        if g == 1:
                            await_(pe, x_done, count(i, 0, 1, 0))
                    else:
                        pe.wait_ge(turned_out, count(i, 0, NG, g - 1))
                    for c, k in enumerate(chunks):
                        mm = pe.transpose(feat_bank[g % 2][:, c * P:(c + 1) * P],
                                          emb[n][:, k, :, :].rearrange("p h d -> p (h d)"), identity[:])
                    if g == NG - 1:
                        pe.wait_ge(dense_got[n], (i // 2 + 1) * 16 if isinstance(i, int) else i[0] * 16 + 16)
                        for k in range(KD):
                            mm = pe.matmul(feat_bank[1][:, P:2 * P], dense_in[n][:, k, :], wd_sb[:, k, :],
                                           start=(k == 0), stop=(k == KD - 1))
                    mm.then_inc(turned, 1)

            def g_product(i, g):
                pe.wait_ge(turned_out, count(i, 0, NG, min(g + 3, NG)))
                if g == 1:
                    pe.wait_ge(x_scaled, count(i, 0, 1, 1))
                if g >= 2:
                    pe.wait_ge(prod_done, count(i, 0, NG, g - 1))
                for c, k in enumerate(GROUPS[g]):
                    mm = pe.matmul(feat_bank[g % 2][:, c * P:(c + 1) * P], emb_t[:, k, :], gram_w[:],
                                   start=True, stop=True)
                if g == NG - 1:
                    mm = pe.transpose(feat_bank[1][:, P:2 * P], x_n[:], identity[:])
                mm.then_inc(g_done, 1)

            def fold(i, m):
                lag = 1 if m else 0
                pe.wait_ge(emb_scaled, count(i, lag, 2, 1 if FOLDS[m][-1][0] < PARTS[0].stop else 2))
                await_(pe, fold_out, count(i, lag, NF, m))
                for n, (k, s, width) in enumerate(FOLDS[m]):
                    c, s0 = s - m * BS, s - samples_of(k)[0]
                    mm = pe.matmul(fold_bank[:, c * PR:(c + width) * PR],
                                   emb_n[:, k, :, :].rearrange("p h d -> p (h d)"),
                                   fold_w[:, k, s0:s0 + width, :].rearrange("p s q -> p (s q)"),
                                   start=(n == 0), stop=(n == len(FOLDS[m]) - 1), skip_group_check=True)
                mm.then_inc(fold_done, 1)

            def project(i, s):
                m, h = divmod(s, 2)
                pe.wait_ge(fold_out, count(i, 1, NF, m + 1))
                pe.wait_ge(fold_again, count(i, 1, NF, m + 1))
                await_(pe, norm_done, count(i, 1, BLOCKS, s - 1))
                y = y_bank[s % 2][:]
                pe.matmul(y, wg_hi[:], folded[:, h, m, :], start=True, stop=False)
                pe.matmul(y, wg_lo[:], folded_b[:, h, m, :], start=False, stop=True).then_inc(y_done, 1)

            def gram(i, lag, s):
                n, u = (parity(i) + lag) % 2, s // 2
                pe.wait_ge(norm_done, count(i, lag, BLOCKS, s + 1))
                if s == 0:
                    pe.wait_ge(x_done, count(i, lag, 1, 1))
                if s % 2 == 0:
                    await_(pe, gram_out, count(i, lag, 4, u - 1))
                for b in range(s * BS, (s + 1) * BS):
                    g, j = divmod(b, 4)
                    c = (g - 2 * u * BS // 4) * TC
                    mm = pe.matmul(gram_bank[u % 2][32 * j:32 * j + 32, c:c + TC], tt[n][:, b, 0:PR],
                                   tt[n][:, b, :], start=True, stop=True)
                if s == BLOCKS - 1:
                    for j in range(4):
                        mm = pe.matmul(gram_bank[1][32 * j:32 * j + 32, 384:384 + GR], ones[:],
                                       tt[n][:, j::4, PR], start=True, stop=True)
                mm.then_inc(gram_done, 1)

            def interact(i, ks):
                if ks[0] == 0:
                    await_(pe, yv_out, count(i, 2, 1, 0))
                    pe.wait_ge(pairs_out, count(i, 2, 1, 1))
                for k in ks:
                    for n, (u, w) in enumerate(((pairs_hi, wl_hi), (pairs_hi, wl_lo), (pairs_lo, wl_hi))):
                        mm = pe.matmul(tower_bank[:], u[:, :, :, k].rearrange("p j g -> p (j g)"),
                                       w[:, k, :], start=(k == 0 and n == 0), stop=(k == QK and n == 2))
                if ks[-1] == QK:
                    mm.then_inc(z_done, 1)

            def turn_z(i):
                pe.wait_ge(z_scaled, count(i, 3, 1, 1))
                for k in range(KO):
                    mm = pe.transpose(tower_bank[:, k * P:(k + 1) * P], z_n[:, k * P:(k + 1) * P], identity[:])
                mm.then_inc(zt_done, 1)

            def hidden1(i, ms):
                first = (i - 3) * P if isinstance(i, int) else pe.snap(i[0] * (2 * P) + (i[1] - 3) * P)
                if ms[0] == 0:
                    pe.wait_ge(z_parts, count(i, 3, 1, 1))
                for m in ms:
                    for k in range(KO + KD):
                        hi = z_hi[:, k, :] if k < KO else dense_hi[:, k - KO, bass.ds(first, P)]
                        lo = z_lo[:, k, :] if k < KO else dense_lo[:, k - KO, bass.ds(first, P)]
                        for n, (w, u) in enumerate(((w1_hi, hi), (w1_lo, hi), (w1_hi, lo))):
                            mm = pe.matmul(tower_bank[:, m * P:(m + 1) * P], w[:, k, m * P:(m + 1) * P], u,
                                           start=(k == 0 and n == 0), stop=(k == KO + KD - 1 and n == 2))
                if ms[-1] == KH1 - 1:
                    mm.then_inc(h1_done, 1)

            def hidden2(i):
                pe.wait_ge(h1_out, count(i, 3, 1, 1))
                for m in range(KH2):
                    for k in range(KH1):
                        mm = pe.matmul(tower_bank[:, m * P:(m + 1) * P], w2_sb[:, k, m * P:(m + 1) * P],
                                       h1_t[:, k, :], start=(k == 0), stop=(k == KH1 - 1))
                mm.then_inc(h2_done, 1)

            def last_layer(i):
                pe.wait_ge(h2_out, count(i, 3, 1, 1))
                for k in range(KH2):
                    mm = pe.matmul(tower_bank[0:1, H2:H2 + P], w3_sb[:, k:k + 1], h2_t[:, k, :],
                                   start=(k == 0), stop=(k == KH2 - 1))
                mm.then_inc(yv_done, 1)

            def step(i, a, c, z, t):
                if i == 2:
                    pe.wait_ge(parts, 1)
                if i == 3:
                    pe.wait_ge(parts, 3)
                for s in range(BLOCKS):
                    if s == 0:
                        if z:
                            gram(i, 2, BLOCKS - 2)
                        if a:
                            turn(i, (0, 1))
                    if c:
                        project(i, s)
                    if s == 0:
                        if t:
                            turn_z(i)
                        if z:
                            gram(i, 2, BLOCKS - 1)
                        if a:
                            turn(i, (2, 3))
                    if c and s in FOLD_SLOT:
                        fold(i, FOLD_SLOT.index(s) + 1)
                    if c and s >= 2:
                        gram(i, 1, s - 2)
                    if a:
                        for g in range(NG):
                            if s == G_SLOT[g]:
                                g_product(i, g)
                    if t and s == 1:
                        hidden1(i, range(KH1))
                    if t and s == 2:
                        hidden2(i)
                    if t and s == 3:
                        last_layer(i)
                    if z and s in (4, 5, 6):
                        interact(i, {4: range(0, 1), 5: range(1, 2), 6: range(2, QK + 1)}[s])
                    if a and s == 6:
                        fold(i, 0)

            run_steps(pe, step)

        @block.scalar
        def _(act):
            act.wait_ge(s_wse_ps, 1)
            act.activation(ws_e[:], bank[0][:, 0:P], ACT.Copy).then_inc(s_wse, 1)
            act.wait_ge(s_gram_ps, 1)
            act.wait_ge(s_const, 1)
            for h in range(2):
                s = slice(h * D, (h + 1) * D)
                act.activation(gram_w[s, s], bank[1][s, s], ACT.Copy, scale=1.0 / E).then_inc(s_gramw, 1)

            def sqrt(dst, src, scale, done, floor=eps):
                act.activation(dst, src, ACT.Sqrt, bias=floor[:], scale=scale).then_inc(done, 1)

            def turn_out(i, groups):
                if groups[0] == 0:
                    await_(act, g_done, count(i, 0, NG, 0))
                for g in groups:
                    act.wait_ge(turned, count(i, 0, NG, g + 1))
                    k, n = GROUPS[g][0], len(GROUPS[g])
                    act.activation(emb_t[:, k:k + n, :].rearrange("p k r -> p (k r)"),
                                   feat_bank[g % 2][:, 0:n * P], ACT.Copy).then_inc(turned_out, 1)

            def x_root(i):
                act.activation(junk_x[:], feat_bank[1][:, P:2 * P], ACT.Square, accum_out=var_x[:]).then_inc(x_sq, 1)
                act.wait_ge(x_sq, count(i, 0, 1, 1))
                sqrt(std_x[:], var_x[:], 1.0 / E, x_std)

            def gram_copy(i, lag, u):
                act.wait_ge(gram_done, count(i, lag, BLOCKS, 2 * u + 2))
                if u == 0:
                    await_(act, regrouped, count(i, lag, 256, 0))
                g = GR // 4
                if u == 3:
                    act.activation(gram_s[:, 2, :, QK], gram_bank[1][:, 384:384 + GR], ACT.Copy)
                src = gram_bank[u % 2][:, 0:g * TC].rearrange("p (g q) -> p g q", q=TC)
                dst = gram_s[:, :, u * g:(u + 1) * g, :]
                act.activation(dst[:, :, :, 0:QK].rearrange("p r g k -> p g k r"),
                               src[:, :, 0:SL].rearrange("p g (k r) -> p g k r", r=4), ACT.Copy)
                act.activation(dst[:, 0:2, :, QK].rearrange("p r g -> p g r"), src[:, :, PR:TC],
                               ACT.Copy).then_inc(gram_low, 1)

            def fold_up(i, m):
                act.wait_ge(fold_done, count(i, 1 if m else 0, NF, m + 1))
                for h in range(2):
                    high = act.activation(folded[0:D, h, m, :], fold_bank[h * D:(h + 1) * D, :], ACT.Copy)
                high.then_inc(fold_high, 1)

            def fold_repeat(i, m):
                act.wait_ge(fold_high, count(i, 1 if m else 0, NF, m + 1))
                act.activation(folded_b[0:D, :, m, :], folded[0:D, :, m, :], ACT.Copy).then_inc(fold_again, 1)

            def root_rows(i, lag, n):
                act.wait_ge(var1_done, count(i, lag, 2, n + 1))
                sqrt(std1[:, PARTS[n], :], var1[:, PARTS[n], :], 1.0, std1_done)

            def step(i, a, c, z, t):
                if a:
                    turn_out(i, (0, 1))
                for s in range(BLOCKS):
                    if c:
                        act.wait_ge(y_done, count(i, 1, BLOCKS, s + 1))
                        await_(act, var_done, count(i, 1, BLOCKS, s - 1))
                        act.activation(square[s % 2][:].rearrange("p s q -> p (s q)"), y_bank[s % 2][:],
                                       ACT.Square).then_inc(sq_done, 1)
                    if t and s == 4:
                        first = (i - 3) * P if isinstance(i, int) else act.snap(i[0] * (2 * P) + (i[1] - 3) * P)
                        act.wait_ge(yv_done, count(i, 3, 1, 1))
                        act.activation(y_all[0:1, bass.ds(first, P)].rearrange("o (g j) -> o j g", j=4),
                                       tower_bank[0:1, H2:H2 + P].rearrange("o (j g) -> o j g", j=4),
                                       ACT.Copy).then_inc(yv_out, 1)
                    if t and s == 2:
                        act.wait_ge(h1_done, count(i, 3, 1, 1))
                        for m in range(KH1):
                            ins = act.activation(h1_t[:, m, :], tower_bank[:, m * P:(m + 1) * P], ACT.Relu,
                                                 bias=b1_sb[:, m:m + 1], scale=1.0 / UP)
                        ins.then_inc(h1_out, 1)
                    if c and s in FOLD_SLOT:
                        fold_up(i, FOLD_SLOT.index(s) + 1)
                    if a and s == 1:
                        act.wait_ge(x_rstd, count(i, 0, 1, 1))
                        act.activation(x_n[:], feat_bank[1][:, P:2 * P], ACT.Copy,
                                       scale=rstd_x[:]).then_inc(x_scaled, 1)
                    if t and s == 3:
                        act.wait_ge(h2_done, count(i, 3, 1, 1))
                        for m in range(KH2):
                            ins = act.activation(h2_t[:, m, :], tower_bank[:, m * P:(m + 1) * P], ACT.Relu,
                                                 bias=b2_sb[:, m:m + 1])
                        ins.then_inc(h2_out, 1)
                    if z and s == 7:
                        act.wait_ge(z_done, count(i, 2, 1, 1))
                        act.activation(junk_z[:], tower_bank[:], ACT.Square, accum_out=var3[:]).then_inc(z_sq, 1)
                    if z and s == 7:
                        act.wait_ge(z_sq, count(i, 2, 1, 1))
                        sqrt(std3[:], var3[:], 1.0 / O, z_std, eps_z)
                    if a and s == 7:
                        fold_repeat(i, 0)
                    if c:
                        act.wait_ge(var_done, count(i, 1, BLOCKS, s + 1))
                        sqrt(std2[s % 2][:], var2[s % 2][:], 1.0 / PR, std_done)
                    if s == 0:
                        if t:
                            act.wait_ge(zt_done, count(i, 3, 1, 1))
                            act.activation(z_hi[:].rearrange("p k b -> p (k b)"), tower_bank[:, 0:OU],
                                           ACT.Copy).then_inc(zt_out, 1)
                        if z:
                            gram_copy(i, 2, 3)
                        if a:
                            turn_out(i, (2, 3))
                            x_root(i)
                    if c and s in FOLD_SLOT:
                        fold_repeat(i, FOLD_SLOT.index(s) + 1)
                    if a and s == VAR_SLOT[0]:
                        root_rows(i, 0, 0)
                    if c and s == VAR_SLOT[1]:
                        root_rows(i, 1, 1)
                    if z and s == 3:
                        act.wait_ge(regrouped, count(i, 2, 256, 256))
                        act.activation(pairs_hi[:], pairs[:], ACT.Copy).then_inc(pairs_high, 1)
                    if c and s in (4, 6):
                        gram_copy(i, 1, (4, 6).index(s))
                    if a and s == 6:
                        fold_up(i, 0)
                    if z and s == 7:
                        act.wait_ge(z_rstd, count(i, 2, 1, 1))
                        act.activation(z_n[:], tower_bank[:, 0:OU], ACT.Copy, scale=rstd3[:]).then_inc(z_scaled, 1)
                if c:
                    gram_copy(i, 1, 2)
                if i == 0:
                    act.wait_ge(s_wl_ready, 1)
                    act.activation(wl_hi[:], wl_sb[:], ACT.Copy, scale=float(UP)).then_inc(highs, 1)
                    act.wait_ge(s_w1_ready, 1)
                    act.activation(w1_hi[:], w1_sb[:], ACT.Copy, scale=float(UP)).then_inc(highs, 1)
                    act.wait_ge(s_dense, 16)
                    for k in range(KD):
                        high = act.activation(by_residue(dense_hi, k), from_sample(k), ACT.Copy)
                    high.then_inc(highs, 1)

            run_steps(act, step)

        @block.vector
        def _(dve):
            done = [0]

            def link(ins):
                done[0] += 1
                ins.then_inc(s_prep, 1)
                dve.wait_ge(s_prep, done[0])

            def centre(w, mean, width):
                link(dve.tensor_reduce(mean, w, AX.X, ALU.add))
                link(dve.tensor_scalar(mean, mean, 1.0 / width, None, ALU.mult))
                link(dve.tensor_tensor(w, w, mean.unsqueeze(2).broadcast_to(list(w.shape)), ALU.subtract))

            dve.wait_ge(s_ids, 32)
            dve.tensor_tensor(ids_all[:].rearrange("p (t c) -> p t c", c=2 * CH),
                              ids_all[:].rearrange("p (t c) -> p t c", c=2 * CH),
                              off_sb[:].unsqueeze(1).broadcast_to([P, TILES, 2 * CH]),
                              ALU.add).then_inc(s_ids_ready, 1)
            dve.memset(eps[:], EPS)
            dve.memset(eps_z[:], EPS * UP * UP)
            dve.memset(ones[:], 1.0)
            dve.memset(tt[0][:, :, PR + 1:TC], 1.0)
            dve.memset(gram_s[:, 3, :, QK], 1.0)
            link(dve.memset(mix_w[:], 0.0))
            dve.memset(gram_w[:], 0.0).then_inc(s_const, 1)
            dve.wait_ge(s_ws, 16 * len(WS))
            centre(ws_sb[:].unsqueeze(1), mean_a[:], E)
            dve.tensor_tensor(wg_sb[:], ws_sb[:], gs_sb[:], ALU.mult).then_inc(s_ws_ready, 1)
            dve.wait_ge(s_wsi, 16 * len(WSI))
            centre(wsi_sb[:], mean_b[:], PR)
            dve.tensor_scalar(mean_a[:], mean_a[:], 1.0, None, ALU.mult).then_inc(s_wsi_ready, 1)
            dve.tensor_tensor(fold_w[:], wsi_sb[:].unsqueeze(2).broadcast_to([P, CH, SPAN, PR]),
                              owner_sb[:].unsqueeze(3).broadcast_to([P, CH, SPAN, PR]),
                              ALU.mult).then_inc(s_fold_ready, 1)
            centre(wd_sb[:], mean_c[:], E)
            dve.tensor_scalar(mean_a[:], mean_a[:], 1.0, None, ALU.mult).then_inc(s_wd_ready, 1)
            dve.wait_ge(s_wsum_ps, 1)
            link(dve.tensor_copy(wsum_row[:], bank[2][0:1, 0:PR].unsqueeze(1).broadcast_to([1, BS, PR])))
            wsum = wsum_row[:].rearrange("o s q -> o (s q)")
            dve.tensor_copy(bs_parts[:, 0, :], bs_row[:])
            dve.tensor_copy(wg_hi[:], wg_sb[:])
            link(dve.tensor_copy(wsum_parts[:, 0, :], wsum))
            dve.tensor_tensor(bs_parts[:, 1, :], bs_row[:], bs_parts[:, 0, :], ALU.subtract)
            dve.tensor_tensor(wg_lo[0:D, :], wg_sb[0:D, :], wg_hi[0:D, :], ALU.subtract)
            dve.tensor_tensor(wsum_parts[:, 1, :], wsum, wsum_parts[:, 0, :], ALU.subtract).then_inc(s_parts, 1)
            dve.wait_ge(s_small, 16 * len(SMALL))
            for dst, u, v in ((gg, gp, gq), (gb, gp, bq), (bg, bp, gq), (bb, bp, bq)):
                link(dve.tensor_scalar(dst[:], v[:], u[:], None, ALU.mult))
            link(dve.tensor_scalar(mix_w[:, 0:QK, 96], bb[:], float(E), None, ALU.mult))
            link(dve.tensor_copy(mix_w[:, QK, 64:65], bp[:]))
            for k in range(QK):
                link(dve.tensor_scalar(mix_w[:, k, PR:2 * PR], eye_p_sb[:], gb[:, k:k + 1], None, ALU.mult))
                link(dve.scalar_tensor_tensor(out=mix_w[:, k, PR:2 * PR], in0=eye_q_sb[:, k, :],
                                              scalar=bg[:, k:k + 1], in1=mix_w[:, k, PR:2 * PR],
                                              op0=ALU.mult, op1=ALU.add))
            dve.wait_ge(s_wl, 16)
            centre(wl_sb[:], mean_d[:], O)
            dve.tensor_scalar(mean_a[:], mean_a[:], 1.0, None, ALU.mult).then_inc(s_mix_ready, 1)
            dve.wait_ge(s_mix_ps, 1)
            for k in range(QK):
                dve.tensor_scalar(wl_sb[:, k, :], wl_sb[:, k, :], gg[:, k:k + 1], None, ALU.mult)
            dve.tensor_scalar(wl_sb[0:PR, QK, :], wl_sb[0:PR, QK, :], gp[0:PR, :], None, ALU.mult)
            for r in (1, 2):
                dve.tensor_copy(wl_sb[r * PR:(r + 1) * PR, QK, :], bank[4][r * PR:(r + 1) * PR, :])
            dve.tensor_copy(wl_sb[3 * PR:P, QK, :], bank[4][3 * PR:P, :]).then_inc(s_wl_ready, 1)
            dve.wait_ge(s_b1_ps, 1)
            for k in range(KO):
                dve.tensor_scalar(w1_sb[:, k, :], w1_sb[:, k, :], gl_sb[:, k:k + 1], None, ALU.mult)
            dve.tensor_tensor(b1_sb[:], b1_sb[:], bank[3][:, 0:KH1], ALU.add).then_inc(s_w1_ready, 1)

            def products(i, g):
                chunks = GROUPS[g]
                dve.wait_ge(g_done, count(i, 0, NG, g + 1))
                sl = slice(chunks[0], chunks[-1] + 1)
                dve.tensor_tensor(prod[:, sl, :, :].rearrange("p k h d -> p (k h d)"),
                                  feat_bank[g % 2][:, 0:len(chunks) * P],
                                  emb[parity(i)][:, sl, :, :].rearrange("p k h d -> p (k h d)"),
                                  ALU.mult).then_inc(prod_done, 1)

            def gram_pick(i, lag, u):
                dve.wait_ge(gram_low, count(i, lag, 4, u + 1))
                dve.tensor_copy(wait_carrier_v[:, u:u + 1], eps[:])
                g = GR // 4
                src = gram_bank[u % 2][:, 0:g * TC].rearrange("p (g q) -> p g q", q=TC)
                dve.copy_predicated(
                    gram_s[:, :, u * g:(u + 1) * g, 0:QK].rearrange("p r g k -> p g k r"),
                    take_upper[:].rearrange("p (k r) -> p k r", r=4).unsqueeze(1).broadcast_to([P, g, QK, 4]),
                    src[:, :, SL:PR].rearrange("p g (k r) -> p g k r", r=4)).then_inc(gram_out, 1)

            def sum_rows(i, lag, n):
                part = PARTS[n]
                dve.wait_ge(prod_done, count(i, lag, NG, 2 * n + 2))
                dve.tensor_reduce(var1[:, part, :], prod[:, part, :, :], AX.X, ALU.add).then_inc(var1_done, 1)

            def scale_rows(i, lag, n):
                part = PARTS[n]
                dve.wait_ge(std1_done, count(i, lag, 2, n + 1))
                dve.reciprocal(rstd1[:, part, :], std1[:, part, :]).then_inc(rstd1_done, 1)
                dve.wait_ge(rstd1_done, count(i, lag, 2, n + 1))
                await_(dve, fold_done, count(i, lag, NF, 0))
                dve.tensor_tensor(emb_n[:, part, :, :], emb[(parity(i) + lag) % 2][:, part, :, :],
                                  rstd1[:, part, :].unsqueeze(3).broadcast_to([P, part.stop - part.start, 2, D]),
                                  ALU.mult).then_inc(emb_scaled, 1)

            def fold_rest(i, m):
                dve.wait_ge(fold_high, count(i, 1 if m else 0, NF, m + 1))
                for h in range(2):
                    low = dve.tensor_tensor(folded[D:P, h, m, :], fold_bank[h * D:(h + 1) * D, :],
                                            folded[0:D, h, m, :], ALU.subtract)
                low.then_inc(fold_out, 1)

            def step(i, a, c, z, t):
                for s in range(BLOCKS):
                    if c:
                        dve.wait_ge(sq_done, count(i, 1, BLOCKS, s + 1))
                        dve.tensor_reduce(var2[s % 2][:], square[s % 2][:], AX.X, ALU.add).then_inc(var_done, 1)
                    if c and s in FOLD_SLOT:
                        fold_rest(i, FOLD_SLOT.index(s) + 1)
                    if a and s == VAR_SLOT[0]:
                        sum_rows(i, 0, 0)
                    if c and s == VAR_SLOT[1]:
                        sum_rows(i, 1, 1)
                    if a and s == SCALE_SLOT[0]:
                        scale_rows(i, 0, 0)
                    if c and s == SCALE_SLOT[1]:
                        scale_rows(i, 1, 1)
                    if z and s == 7:
                        dve.wait_ge(z_std, count(i, 2, 1, 1))
                        dve.reciprocal(rstd3[:], std3[:]).then_inc(z_rstd, 1)
                    if c:
                        dve.wait_ge(std_done, count(i, 1, BLOCKS, s + 1))
                        dve.reciprocal(rstd2[s % 2][:], std2[s % 2][:]).then_inc(rstd_done, 1)
                        dve.wait_ge(rstd_done, count(i, 1, BLOCKS, s + 1))
                        dve.tensor_tensor(tt[parity(i) ^ 1][:, s * BS:(s + 1) * BS, 0:PR],
                                          y_bank[s % 2][:].rearrange("p (s q) -> p s q", q=PR),
                                          rstd2[s % 2][:].unsqueeze(2).broadcast_to([P, BS, PR]),
                                          ALU.mult).then_inc(norm_done, 1)
                    if s == 0:
                        if t:
                            dve.wait_ge(zt_out, count(i, 3, 1, 1))
                            dve.tensor_tensor(z_lo[:].rearrange("p k b -> p (k b)"), tower_bank[:, 0:OU],
                                              z_hi[:].rearrange("p k b -> p (k b)"), ALU.subtract).then_inc(z_parts, 1)
                        if z:
                            gram_pick(i, 2, 3)
                        if a:
                            dve.wait_ge(x_std, count(i, 0, 1, 1))
                            dve.reciprocal(rstd_x[:], std_x[:]).then_inc(x_rstd, 1)
                    if a:
                        for g in range(NG):
                            if s == G_SLOT[g]:
                                products(i, g)
                                if g == NG - 1:
                                    await_(dve, gram_done, count(i, 1, BLOCKS, 0))
                                    dve.tensor_scalar(tt[parity(i)][:, :, PR], feat_bank[1][:, P:2 * P],
                                                      gd_sb[:], bd_sb[:], ALU.mult, ALU.add).then_inc(x_done, 1)
                    if z and s == 3:
                        dve.wait_ge(pairs_high, count(i, 2, 1, 1))
                        dve.tensor_tensor(pairs_lo[:], pairs[:], pairs_hi[:], ALU.subtract).then_inc(pairs_out, 1)
                    if c and s in (4, 6):
                        gram_pick(i, 1, (4, 6).index(s))
                    if a and s == 6:
                        fold_rest(i, 0)
                if c:
                    gram_pick(i, 1, 2)
                if i == 0:
                    for n, (low, w, high) in enumerate(((wl_lo, wl_sb, wl_hi), (w1_lo, w1_sb, w1_hi))):
                        dve.wait_ge(highs, n + 1)
                        dve.scalar_tensor_tensor(out=low[:], in0=w[:], scalar=float(UP), in1=high[:],
                                                 op0=ALU.mult, op1=ALU.subtract).then_inc(parts, 1)
                    dve.wait_ge(highs, 3)
                    for k in range(KD):
                        low = dve.tensor_tensor(by_residue(dense_lo, k), from_sample(k), by_residue(dense_hi, k),
                                                ALU.subtract)
                    low.then_inc(parts, 1)
                    dve.wait_ge(parts, 3)
                    dve.memset(tt[1][:, :, PR + 1:TC], 1.0)

            run_steps(dve, step)


def kernel(**inputs):
    from concourse import bacc
    from concourse.bass_utils import run_bass_kernel_spmd

    a = {k: np.asarray(v) for k, v in inputs.items()}
    row = np.arange(CH * P).reshape(CH, P)
    feat = (row % NS).T
    owner = (row // NS).T - (np.arange(CH) * P // NS)[None, :]
    base = np.concatenate([[0], np.cumsum(VOCAB)[:-1]])
    by_half = a["ids"].astype(np.int32, copy=False).reshape(TILES, NF, 2, BS * NS).transpose(0, 2, 1, 3)
    by_chunk = by_half.reshape(TILES, 2, CH, P).transpose(3, 0, 2, 1)
    offsets = np.repeat(base[feat][:, :, None], 2, axis=2).reshape(P, 2 * CH)

    pr = np.arange(P)[:, None] % PR
    slot = 4 * np.arange(QK)[None, :] + (np.arange(P) // PR)[:, None]
    far = (pr % SL < slot) == (pr >= SL)
    q = slot + SL * far
    wl_t = a["L0_rec_Wl"].T
    wl = np.zeros((P, QK + 1, O), wl_t.dtype)
    hi, lo = np.maximum(pr, q) + 1, np.minimum(pr, q) + 1
    rr, kk = np.nonzero((pr % SL != slot) | (pr < SL))
    wl[rr, kk] = wl_t[(hi * (hi - 1) // 2 + lo)[rr, kk]]
    row_p, all_slots = np.arange(P)[:, None] % PR, np.arange(SL)[None, :]
    upper = (row_p % SL < all_slots) == (row_p >= SL)
    pr = pr[:, 0]
    first = np.arange(1, PR + 1)
    wl[0:PR, QK] = wl_t[first * (first - 1) // 2]

    def cols(v, n):
        return v.reshape(n, P).T

    f = np.float32
    args = {
        "table": np.concatenate([a[f"tbl_{n}"] for n in range(NS)]),
        "ids": by_chunk.reshape(P, TILES * 2 * CH),
        "offsets": offsets.astype(np.int32),
        "dense_t": a["r_dense_t"].T,
        "ident": np.eye(P, dtype=f),
        "ws_t": np.concatenate([a["L0_rec_Ws"].T] * 2),
        "gs": np.broadcast_to(a["L0_rec_gs"], (P, E)),
        "bs": a["L0_rec_bs"][None],
        "wsi": a["L0_rec_Wsi"].T[feat],
        "owner": (owner[:, :, None] == np.arange(SPAN)).astype(f),
        "wd_t": a["L0_rec_Wd"].T.reshape(KD, P, E).transpose(1, 0, 2),
        "gd": a["L0_rec_gd"][:, None], "bd": a["L0_rec_bd"][:, None],
        "wl": wl,
        "gsi_p": a["L0_rec_gsi"][pr][:, None], "gsi_q": a["L0_rec_gsi"][q],
        "bsi_p": a["L0_rec_bsi"][pr][:, None], "bsi_q": a["L0_rec_bsi"][q],
        "eye_p": (pr[:, None] == np.arange(PR)).astype(f),
        "eye_q": (q[:, :, None] == np.arange(PR)).astype(f),
        "w1": np.concatenate([a["W_top1"][:OU], a["W_top1"][O:]]).reshape(KO + KD, P, H1).transpose(1, 0, 2),
        "gl": cols(a["L0_rec_gl"][:OU], KO), "bl": cols(a["L0_rec_bl"][:OU], KO),
        "b1": cols(a["b_top1"], KH1),
        "w2": a["W_top2"].reshape(KH1, P, H2).transpose(1, 0, 2),
        "b2": cols(a["b_top2"], KH2),
        "upper": upper.astype(np.int32),
        "w3": a["W_top3"].reshape(KH2, P).T,
    }
    nc = bacc.Bacc("TRN2", target_bir_lowering=False, num_devices=1)
    args = {k: np.ascontiguousarray(v) for k, v in args.items()}
    aps = {k: nc.dram_tensor(f"in_{k}", v.shape, mybir.dt.from_np(v.dtype), kind="ExternalInput").ap()
           for k, v in args.items()}
    out = nc.dram_tensor("out_y", (B, 1), F32, kind="ExternalOutput").ap()
    build_tower(nc, **aps, out=out)
    r = run_bass_kernel_spmd(nc, [{f"in_{k}": v for k, v in args.items()}], core_ids=[0])
    return r.results[0]["out_y"]
```
